# Optimizing a Trainium2 kernel written in Bass

```python
import numpy as np
import jax
import jax.numpy as jnp

def _softmax(x, axis=-1):
    return jax.nn.softmax(x, axis=axis)

def _gelu(x):
    return jax.nn.gelu(x, approximate=True)

def _silu(x):
    return jax.nn.silu(x)

def _sigmoid(x):
    return jax.nn.sigmoid(x)

def _layernorm(x, axis=-1, eps=1e-05):
    m = jnp.mean(x, axis=axis, keepdims=True)
    v = jnp.var(x, axis=axis, keepdims=True)
    return (x - m) / jnp.sqrt(v + eps)

def _scatter_add(tgt, idx, src, axis=0):
    return tgt.at[idx].add(src)

def _segment_sum(src, seg, n):
    return jax.ops.segment_sum(src, seg, n)
kernel_name = 'mk_prb_d1_jaxref_r4_e2324d'

def setup_inputs(seed: int=0):
    np.random.seed(seed)
    _w = jnp.asarray

    def _L0_attn_setup():
        import jax, jax.numpy as jnp
        import numpy as np
        import math
        N_HEADS = 16
        DIM = 256
        B, S = (2, 512)

        def _split_heads(x, n_heads):
            b, s, d = x.shape
            dh = d // n_heads
            return x.reshape(b, s, n_heads, dh).transpose(0, 2, 1, 3)
        key = jax.random.key(seed)
        ks = jax.random.split(key, 9)
        std = 0.02
        inp = {'query': jax.random.normal(ks[0], (B, S, DIM), dtype=jnp.float32), 'mask': jnp.ones((B, S), dtype=jnp.int64), 'q_w': jax.random.normal(ks[1], (DIM, DIM), dtype=jnp.float32) * std, 'q_b': jnp.zeros((DIM,), dtype=jnp.float32), 'k_w': jax.random.normal(ks[2], (DIM, DIM), dtype=jnp.float32) * std, 'k_b': jnp.zeros((DIM,), dtype=jnp.float32), 'v_w': jax.random.normal(ks[3], (DIM, DIM), dtype=jnp.float32) * std, 'v_b': jnp.zeros((DIM,), dtype=jnp.float32), 'out_w': jax.random.normal(ks[4], (DIM, DIM), dtype=jnp.float32) * std, 'out_b': jnp.zeros((DIM,), dtype=jnp.float32)}
        return inp
    _L0_attn_in = _L0_attn_setup()

    def _L0_ffn_setup():
        import jax, jax.numpy as jnp
        import numpy as np
        FP8_MAX = 448.0

        def quant_fp8(x):
            amax = jnp.max(jnp.abs(x)).astype(jnp.float32)
            scale = jnp.minimum(FP8_MAX / jnp.maximum(amax, 1e-12), FP8_MAX)
            x_fp8 = jnp.clip(x * scale, -FP8_MAX, FP8_MAX).astype(jnp.float8_e4m3fn)
            return (x_fp8, 1.0 / scale)
        key = jax.random.key(seed)
        k1, k2, k3 = jax.random.split(key, 3)
        B, S, IN, OUT = (4, 2048, 256, 256)
        input = jax.random.normal(k1, (B, S, IN), dtype=jnp.float32)
        bound = 1.0 / np.sqrt(IN)
        weight = jax.random.uniform(k2, (OUT, IN), dtype=jnp.float32, minval=-bound, maxval=bound)
        bias = jax.random.uniform(k3, (OUT,), dtype=jnp.float32, minval=-bound, maxval=bound)
        return {'input': input, 'weight': weight, 'bias': bias}
    _L0_ffn_in = _L0_ffn_setup()
    _d = {'L0_attn_query': _L0_attn_in['query'], 'L0_attn_mask': _L0_attn_in['mask'], 'L0_attn_q_w': _L0_attn_in['q_w'], 'L0_attn_q_b': _L0_attn_in['q_b'], 'L0_attn_k_w': _L0_attn_in['k_w'], 'L0_attn_k_b': _L0_attn_in['k_b'], 'L0_attn_v_w': _L0_attn_in['v_w'], 'L0_attn_v_b': _L0_attn_in['v_b'], 'L0_attn_out_w': _L0_attn_in['out_w'], 'L0_attn_out_b': _L0_attn_in['out_b'], 'L0_ffn_weight': _L0_ffn_in['weight'], 'L0_ffn_bias': _L0_ffn_in['bias']}
    _x0 = _d['L0_attn_query']
    _d['L0_attn_query'] = jax.random.normal(jax.random.fold_in(jax.random.key(seed), 1), (1, 4096, 256), dtype=_x0.dtype)
    del _x0
    return _d

def reference(L0_attn_query, L0_attn_mask, L0_attn_q_w, L0_attn_q_b, L0_attn_k_w, L0_attn_k_b, L0_attn_v_w, L0_attn_v_b, L0_attn_out_w, L0_attn_out_b, L0_ffn_weight, L0_ffn_bias):

    def _L0_attn_ref(query, mask, q_w, q_b, k_w, k_b, v_w, v_b, out_w, out_b):
        import jax, jax.numpy as jnp
        import numpy as np
        import math
        N_HEADS = 16
        DIM = 256
        B, S = (2, 512)

        def _split_heads(x, n_heads):
            b, s, d = x.shape
            dh = d // n_heads
            return x.reshape(b, s, n_heads, dh).transpose(0, 2, 1, 3)
        b, s, d = query.shape
        h = N_HEADS
        dh = d // h
        scale = math.sqrt(dh)
        q = _split_heads(query @ q_w.T + q_b, h) / scale
        k = _split_heads(query @ k_w.T + k_b, h)
        v = _split_heads(query @ v_w.T + v_b, h)
        scores = jnp.einsum('bhqd,bhkd->bhqk', q, k)
        attn = jax.nn.softmax(scores.astype(jnp.float32), axis=-1).astype(query.dtype)
        ctx = jnp.einsum('bhqk,bhkd->bhqd', attn, v)
        ctx = ctx.transpose(0, 2, 1, 3).reshape(b, s, d)
        out = ctx @ out_w.T + out_b
        return out

    def _L0_ffn_ref(input, weight, bias):
        import jax, jax.numpy as jnp
        import numpy as np
        FP8_MAX = 448.0

        def quant_fp8(x):
            amax = jnp.max(jnp.abs(x)).astype(jnp.float32)
            scale = jnp.minimum(FP8_MAX / jnp.maximum(amax, 1e-12), FP8_MAX)
            x_fp8 = jnp.clip(x * scale, -FP8_MAX, FP8_MAX).astype(jnp.float8_e4m3fn)
            return (x_fp8, 1.0 / scale)
        prev_shape = input.shape
        x2d = input.reshape(-1, weight.shape[1])
        w_fp8, w_scale = quant_fp8(weight)
        x_fp8, x_scale = quant_fp8(x2d)
        acc = jnp.matmul(x_fp8.astype(jnp.float32), w_fp8.astype(jnp.float32).T)
        out2d = (acc * (x_scale * w_scale) + bias).astype(jnp.bfloat16)
        out = out2d.reshape(*prev_shape[:-1], weight.shape[0]).astype(input.dtype)
        return out
    x = L0_attn_query
    xn = _layernorm(x, axis=-1)
    x = x + _L0_attn_ref(xn, L0_attn_mask, L0_attn_q_w, L0_attn_q_b, L0_attn_k_w, L0_attn_k_b, L0_attn_v_w, L0_attn_v_b, L0_attn_out_w, L0_attn_out_b) + _L0_ffn_ref(xn, L0_ffn_weight, L0_ffn_bias)
    return x

_drawn_inputs = setup_inputs


def setup_inputs(seed=0):
    import zlib

    import numpy as np

    out = dict(_drawn_inputs(seed))
    spreads = {'L0_attn_q_b': (0.0, 0.8),
     'L0_attn_k_b': (0.0, 0.8),
     'L0_attn_v_b': (0.0, 0.316),
     'L0_attn_out_b': (0.0, 0.1)}
    factors = {'L0_attn_q_w': 8.0, 'L0_attn_k_w': 8.0, 'L0_attn_v_w': 8.0}
    for name, (base, spread) in spreads.items():
        noise = np.random.default_rng([zlib.crc32(name.encode()), seed]).standard_normal(out[name].shape)
        drawn = base * np.exp(spread * noise) if base else spread * noise
        out[name] = jnp.asarray(drawn.astype(out[name].dtype))
    for name, factor in factors.items():
        out[name] = (out[name] * factor).astype(out[name].dtype)
    return out
```

```python
from contextlib import ExitStack

import concourse.bass as bass
from concourse import mybir

ALU = mybir.AluOpType
ACT = mybir.ActivationFunctionType
AX = mybir.AxisListType
F32 = mybir.dt.float32
BF16 = mybir.dt.bfloat16
I32 = mybir.dt.int32

P = 128
HEADS = 16
EPS = 1e-5
FP8_MAX = 448.0
FP8_MIN_NORMAL = 2.0 ** -6
ROUND_TO_3_BITS = 1.5 * 2.0 ** 20
EXPONENT_BITS = 0x7F800000
PARTS = 3
TERMS = 6
LAG = 2
SLOTS = 4
VCOLS = 32


def program(nc, x, wq, bq, wk, bk, wv, bv, wo, bo, wf, bf, out):
    _, S, D = x.shape
    DH = D // HEADS
    KD = D // P
    NT = S // P
    CHUNK = 512
    CT = CHUNK // P
    NCH = S // CHUNK
    QB = 4
    UQ = QB * CHUNK
    UNITS = S // UQ
    KT = S // P
    STEPS = UNITS * KT
    UT = UQ // P
    KROWS = TERMS * DH
    STACK = KROWS + PARTS
    NB = 3
    AK = 128
    SCALE = float(DH) ** -0.5
    NH1 = HEADS + 1
    assert (KD, UNITS, DH, TERMS * DH) == (2, 2, 16, 96)

    q_dram = nc.dram_tensor("q_parts", [PARTS, NH1 * DH, S], BF16, kind="Internal").ap()
    k_dram = nc.dram_tensor("k_parts", [PARTS, NH1 * DH, S], BF16, kind="Internal").ap()
    xnT_dram = nc.dram_tensor("xnT_copy", [P, KD, S], F32, kind="Internal").ap()

    with ExitStack() as ctx:
        def sb(name, shape, dt=F32):
            return ctx.enter_context(nc.sbuf_tensor(name, shape, dt))

        def sem(name):
            return ctx.enter_context(nc.semaphore(name))

        x_all = sb("x_all", [P, NT, D])
        xn_all = sb("xn_all", [P, NT, D])
        ctx_all = xn_all
        v_all = sb("v_all", [P, NT, D])
        w_sb = {n: sb(f"w_{n}", [P, KD, D]) for n in "qkvof"}
        qk_bias = sb("qk_bias", [P, 2, KD])
        bv_sb = sb("bv_sb", [P, 2, D])
        bo_sb = sb("bo_sb", [P, 2, D])
        bf_sb = sb("bf_sb", [P, 2, D])
        ident = sb("ident", [P, P])
        ident_bf = sb("ident_bf", [P, P], BF16)
        ones = sb("ones", [P, 1])
        stats = sb("stats", [P, 8, 6])
        mean_var = sb("mean_var", [P, NT, 2])
        ln = sb("ln", [P, 5, NT])
        amax = sb("amax", [P, 2, 8])
        amax_all = sb("amax_all", [P, 2])
        fscale = sb("fscale", [P, 2, 4])
        out_scale = sb("out_scale", [P, 1])
        parts = [sb(f"parts{i}", [P, PARTS, CHUNK], BF16) for i in range(4)]
        q_st = sb("q_st", [STACK, S], BF16)
        k_st = sb("k_st", [STACK, S], BF16)
        v_st = sb("v_st", [P, KT, VCOLS])
        probs = sb("probs", [P, SLOTS, UQ])
        xnc = [probs[:, i, 0:CT * D].rearrange("p (t d) -> p t d", t=CT) for i in range(2)]
        xnTc = [probs[:, 2 + i, 0:KD * CHUNK].rearrange("p (k c) -> p k c", k=KD) for i in range(2)]
        mcol = sb("mcol", [P, UT])
        mpart = sb("mpart", [P, S // CHUNK])
        neg = sb("neg", [P, P // UT, UT], BF16)
        neg_rest = sb("neg_rest", [P, UT])
        neg_row = sb("neg_row", [PARTS * UT, P], BF16)
        o_sb = sb("o_sb", [P, CHUNK])
        o_junk = sb("o_junk", [P, CHUNK])
        o_inf = sb("o_inf", [P, UNITS * HEADS])
        rden = sb("rden", [P, UT])
        all_ok = sb("all_ok", [P, 2])
        flag = sb("flag", [1, 1], I32)
        rest = [o_sb, o_junk]
        xq = w_sb["f"][:, :, :].rearrange("p k n -> p (k n)")
        qt = [sb("qt0", [P, CHUNK]), sb("qt1", [P, CHUNK]), o_junk]
        x8T = sb("x8T", [P, KD, S], BF16)
        w8T = sb("w8T", [P, KD, D], BF16)
        cx = xnc[0]
        ctxT = xnTc[0]
        y_sb = [parts[i][:, 0, :] for i in range(2)]
        res = rest
        o_out = [qt[0], qt[1]]

        banks = ctx.enter_context(nc.psum_tensor("banks", [P, 8, CHUNK], F32))
        acc = banks[:, 6, :]
        misc = banks[:, 7, :]

        x_in = [sem(f"x_in{i}") for i in range(4)]
        w_in = {n: sem(f"w_in_{n}") for n in "qkvof"}
        bias_in = sem("bias_in")
        consts = sem("consts")
        ln_chain = sem("ln_chain")
        var_ready = sem("var_ready")
        root_ready = sem("root_ready")
        xn_ready = sem("xn_ready")
        amax_ready = sem("amax_ready")
        amax_shared = sem("amax_shared")
        xnc_ready = sem("xnc_ready")
        turned = sem("turned")
        xT_ready = sem("xT_ready")
        xT_saved = [sem(f"xT_saved{i}") for i in range(2)]
        qk_done = sem("qk_done")
        hi_done = sem("hi_done")
        rest_done = sem("rest_done")
        mid_done = sem("mid_done")
        lo_done = sem("lo_done")
        parts_saved = [sem(f"parts_saved{i}") for i in range(4)]
        v_mm = sem("v_mm")
        v_done = sem("v_done")
        flag_ok = sem("flag_ok")
        flag_sum = sem("flag_sum")
        flag_ready = sem("flag_ready")
        pass2_end = sem("pass2_end")
        cx_ready = sem("cx_ready")
        c_turned = sem("c_turned")
        cT_ready = sem("cT_ready")
        ffn_done = sem("ffn_done")
        proj_done = sem("proj_done")
        y_done = sem("y_done")
        res_done = sem("res_done")
        out_ready = sem("out_ready")
        out_saved = [sem(f"out_saved{i}") for i in range(2)]
        xq_in = sem("xq_in")
        xq_used = sem("xq_used")
        quant_chain = sem("quant_chain")

        class Pass:

            def __init__(self, tag, full):
                self.full = full
                self.q_in = [sem(f"{tag}_q_in{i}") for i in range(2)]
                self.k_in = [sem(f"{tag}_k_in{i}") for i in range(2)]
                self.row_in = [sem(f"{tag}_row_in{i}") for i in range(2)]
                self.v_in = [sem(f"{tag}_v_in{i}") for i in range(2)]
                self.st_done = sem(f"{tag}_st_done")
                self.exp_done = sem(f"{tag}_exp_done")
                self.pv_done = sem(f"{tag}_pv_done")
                self.acc_free = sem(f"{tag}_acc_free")
                self.misc_full = sem(f"{tag}_misc_full")
                self.misc_free = sem(f"{tag}_misc_free")
                self.neg_ready = sem(f"{tag}_neg_ready")
                self.row_ready = sem(f"{tag}_row_ready")
                self.chain = sem(f"{tag}_chain")
                self.max_jobs = UT * (S // CHUNK) if full else UT // 4
                self.head_jobs = 2 * (self.max_jobs + 2)

        first = Pass("a", False)
        second = Pass("b", True)

        XNC_0, XT_0, SAVED_0, REST_0, LO_0, V_0 = 4, 2, 16, 4, 4, 2
        PARTS_SAVED = [32, 32, 16, 16]
        EXP_0 = 2 * STEPS
        PV_0 = STEPS
        ACC_0 = 1
        OUT_0 = 16

        tok = "(t p) d -> p t d"
        x_v = x.rearrange("b s d -> (b s) d").rearrange(tok, p=P)
        out_v = out.rearrange("b s d -> (b s) d").rearrange(tok, p=P)

        block = ctx.enter_context(nc.Block())

        @block.sync
        def _(sp):
            wn = {"q": wq, "k": wk, "v": wv, "o": wo, "f": wf}

            def load_w(n):
                sp.dma_start(w_sb[n][:, :, :], wn[n].rearrange("(k p) n -> p k n", p=P)).then_inc(w_in[n], 16)

            load_w("f")
            for g in range(4):
                sp.dma_start(x_all[:, 8 * g:8 * g + 8, :], x_v[:, 8 * g:8 * g + 8, :]).then_inc(x_in[g], 16)
                if g == 0:
                    load_w("q")
                    load_w("k")
            load_w("v")
            load_w("o")
            for i, b in enumerate((bq, bk)):
                sp.dma_start(qk_bias[:, i, :], b.rearrange("(k p) -> p k", p=P),
                             allow_slow_non_contiguous=True).then_inc(bias_in, 16)
            for t, b in ((bv_sb, bv), (bo_sb, bo), (bf_sb, bf)):
                for i in range(2):
                    sp.dma_start(t[:, i, :], b.partition_broadcast(P)
                                 ).then_inc(bias_in, 16)

            for s, n in ((turned, XNC_0), (xT_ready, XT_0), (xT_saved[0], SAVED_0), (xT_saved[1], SAVED_0),
                         (rest_done, REST_0), (lo_done, LO_0), (v_done, V_0), (xq_used, 1),
                         (y_done, 2), (res_done, 2), (out_ready, 2), (out_saved[0], OUT_0), (out_saved[1], OUT_0), (c_turned, 1)):
                sp.sem_inc(s, n)
            for i in range(4):
                sp.sem_inc(parts_saved[i], PARTS_SAVED[i])
            for c in (first, second):
                sp.sem_inc(c.exp_done, EXP_0)
                sp.sem_inc(c.pv_done, PV_0)
                sp.sem_inc(c.acc_free, ACC_0)

            with sp.Fori(0, NCH // 2) as cc:
                for par in range(2):
                    n = cc * 2 + par
                    sp.wait_ge(xT_ready, n * 2 + (XT_0 + 2))
                    sp.wait_ge(lo_done, n * 4 + (LO_0 + 1))
                    sp.dma_start(xnT_dram[:, :, bass.ds(n * CHUNK, CHUNK)], xnTc[par][:, :, :]
                                 ).then_inc(xT_saved[par], 16)
                    for o in range(4):
                        half, which = divmod(o, 2)
                        dram = (q_dram, k_dram)[which]
                        if o:
                            sp.wait_ge(lo_done, n * 4 + (LO_0 + o + 1))
                        cols = bass.ds(n * CHUNK, CHUNK)
                        sp.dma_start(dram[:, half * P:(half + 1) * P, cols].rearrange("a r c -> r a c"),
                                     parts[o][:, :, :]).then_inc(parts_saved[o], 16)
                        if half == 0:
                            sp.dma_start(dram[:, HEADS * DH:NH1 * DH, cols].rearrange("a r c -> r a c"),
                                         parts[o][0:DH, :, :]).then_inc(parts_saved[o], 16)
            for o in range(4):
                sp.wait_ge(parts_saved[o], PARTS_SAVED[o] * (NCH + 1))
            for i in range(2):
                sp.wait_ge(xT_saved[i], SAVED_0 + 16 * (NCH // 2))

            def load_q(c, head, u):
                rows, cols = bass.ds(head * DH, DH), slice(u * UQ, (u + 1) * UQ)
                at = 0
                for a in (3, 2, 1):
                    for i in range(a):
                        sp.dma_start(q_st[at:at + DH, cols], q_dram[i, rows, cols]).then_inc(c.q_in[u], 16)
                        at += DH

            def load_k(c, head, half):
                rows, cols = bass.ds(head * DH, DH), slice(half * (S // 2), (half + 1) * (S // 2))
                for at, i in enumerate((0, 0, 0, 1, 1, 2)):
                    sp.dma_start(k_st[at * DH:(at + 1) * DH, cols], k_dram[i, rows, cols]).then_inc(c.k_in[half], 16)

            def load_rows(c, u, count):
                sp.wait_ge(c.row_ready, count)
                for i in range(PARTS):
                    sp.dma_start(q_st[KROWS + i:KROWS + i + 1, u * UQ:(u + 1) * UQ]
                                 .rearrange("o (t c) -> o t c", c=P),
                                 neg_row[i * UT:(i + 1) * UT, :]).then_inc(c.row_in[u], 16)

            def attend(c):
                for u in range(2):
                    load_q(c, 0, u)
                    load_k(c, 0, u)
                load_rows(c, 0, 1)
                with sp.Fori(0, HEADS) as h:
                    nxt = sp.snap(h + 1)
                    if not c.full:
                        sp.wait_ge(xq_used, h + 1)
                        half_cols = xnT_dram.rearrange("p k s -> p (k s)")
                        sp.dma_start(xq, half_cols[:, bass.ds(h * CHUNK, CHUNK)]).then_inc(xq_in, 16)
                    load_rows(c, 1, h * 2 + 2)
                    sp.wait_ge(c.st_done, h * (2 * STEPS) + 2 * KT)
                    load_q(c, nxt, 0)
                    sp.wait_ge(c.st_done, h * (2 * STEPS) + 2 * (KT + KT // 2))
                    load_k(c, nxt, 0)
                    if not c.full:
                        load_rows(c, 0, h * 2 + 3)
                    sp.wait_ge(c.st_done, h * (2 * STEPS) + 2 * STEPS)
                    load_k(c, nxt, 1)
                    load_q(c, nxt, 1)
                    if c.full:
                        load_rows(c, 0, h * 2 + 3)
                for u in range(2):
                    sp.wait_ge(c.q_in[u], 16 * TERMS * NH1)
                    sp.wait_ge(c.k_in[u], 16 * TERMS * NH1)

            attend(first)
            sp.wait_ge(flag_ready, 1)
            ok = sp.value_load(flag[0:1, 0:1], min_val=0, max_val=P)
            with sp.If(ok < P):
                attend(second)
                sp.wait_ge(pass2_end, 3)

            with sp.Fori(0, NT // 4) as g:
                for b in range(2):
                    sp.wait_ge(out_ready, g * 2 + (b + 1 + 2))
                    sp.dma_start(out_v[:, bass.ds(g * 4 + 2 * b, 2), :],
                                 o_out[b][:, :].rearrange("p (t d) -> p t d", t=2)).then_inc(out_saved[b], 16)
            for b in range(2):
                sp.wait_ge(out_saved[b], OUT_0 + 16 * (NT // 4))

        @block.gpsimd
        def _(pool):
            count = [0]

            def constant(ins):
                count[0] += 1
                ins.then_inc(consts, 1)
                pool.wait_ge(consts, count[0])

            constant(pool.memset(ident[:, :], 0.0))
            constant(pool.affine_select(out=ident[:, :], in_=ident[:, :], compare_op=ALU.not_equal, fill=1.0, base=0,
                                        pattern=[[-1, P]], channel_multiplier=1))
            constant(pool.tensor_copy(ident_bf[:, :], ident[:, :]))
            constant(pool.memset(v_st[:, :, :], 0.0))
            constant(pool.memset(v_st[:, :, DH:DH + 1], 1.0))
            constant(pool.memset(k_st[KROWS:STACK, :], 1.0))
            constant(pool.memset(ones[:, :], 1.0))
            constant(pool.memset(neg[:, :, :], 0.0))

            RMAX = bass.bass_isa.ReduceOp.max
            pool.wait_ge(amax_ready, 1)
            pool.partition_all_reduce(amax_all[:, 1:2], amax[:, 1, 0:1], P, RMAX).then_inc(amax_shared, 1)

            with pool.Fori(0, NCH // 2) as cc:
                pool.wait_ge(xn_ready, cc + 1)
                for par in range(2):
                    n = cc * 2 + par
                    pool.wait_ge(turned, n * 2 + XNC_0 - 2)
                    pool.tensor_copy(xnc[par][:, :, :], xn_all[:, bass.ds(n * CT, CT), :]).then_inc(xnc_ready, 1)
            pool.wait_ge(amax_ready, 2)
            pool.partition_all_reduce(amax_all[:, 0:1], amax[:, 0, 7:8], P, RMAX).then_inc(amax_shared, 1)
            pool.wait_ge(v_done, V_0 + 2 * NCH)

            def attend(c):
                with pool.Fori(0, HEADS) as h:
                    for half in range(2):
                        pool.wait_ge(c.pv_done, h * STEPS + (PV_0 - STEPS) + KT + (half + 1) * (KT // 2))
                        rows = slice(half * (KT // 2), (half + 1) * (KT // 2))
                        pool.tensor_copy(v_st[:, rows, 0:DH], v_all[:, rows, bass.ds(h * DH, DH)]
                                         ).then_inc(c.v_in[half], 1)

            attend(first)
            pool.wait_ge(flag_ready, 1)
            ok = pool.value_load(flag[0:1, 0:1], min_val=0, max_val=P)
            with pool.If(ok < P):
                attend(second)
                pool.wait_ge(pass2_end, 3)

            with pool.Fori(0, NT // 4) as g:
                pool.wait_ge(c_turned, g + 1)
                pool.tensor_copy(cx[:, :, :], ctx_all[:, bass.ds(g * 4, 4), :]).then_inc(cx_ready, 1)

        @block.scalar
        def _(act):
            for g in range(4):
                act.wait_ge(var_ready, g + 1)
                cols = slice(8 * g, 8 * g + 8)
                act.activation(ln[:, 1, cols], ln[:, 0, cols], ACT.Sqrt).then_inc(root_ready, 1)

            act.wait_ge(bias_in, 16 * 8)
            with act.Fori(0, NCH // 2) as cc:
                for par in range(2):
                    n = cc * 2 + par
                    act.wait_ge(xT_saved[par], cc * 16 + SAVED_0)
                    for k in range(KD):
                        act.wait_ge(turned, n * 2 + (XNC_0 + k + 1))
                        act.activation(xnTc[par][:, k, :], banks[:, k, :], ACT.Copy).then_inc(xT_ready, 1)

                    def high(o):
                        half, which = divmod(o, 2)
                        act.wait_ge(parts_saved[o], (n + 1) * PARTS_SAVED[o])
                        act.wait_ge(qk_done, n * 4 + (o + 1))
                        act.activation(parts[o][:, 0, :], banks[:, 2 + o, :], ACT.Identity,
                                       bias=qk_bias[:, which, half:half + 1]).then_inc(hi_done, 1)

                    def middle(o):
                        act.wait_ge(rest_done, n * 4 + (REST_0 + o + 1))
                        act.activation(parts[o][:, 1, :], rest[o % 2][:, :], ACT.Copy).then_inc(mid_done, 1)

                    high(0)
                    high(1)
                    middle(0)
                    high(2)
                    middle(1)
                    high(3)
                    middle(2)
                    middle(3)

            def attend(c):
                def exps(h, t):
                    for a in range(2):
                        i = 2 * t + a
                        buf = i % NB
                        act.wait_ge(c.st_done, h * (2 * STEPS) + (i + 1))
                        if a == 0:
                            act.wait_ge(c.pv_done, h * STEPS + (PV_0 + t - SLOTS + 1))
                        act.activation(probs[:, t % SLOTS, a * 2 * CHUNK:(a + 1) * 2 * CHUNK],
                                       banks[:, 2 * buf:2 * buf + 2, :], ACT.Exp, scale=SCALE
                                       ).then_inc(c.exp_done, 1)

                with act.Fori(0, HEADS) as h:
                    for t in range(STEPS):
                        exps(h, t)
                for t in range(LAG):
                    exps(HEADS, t)

            attend(first)
            act.wait_ge(flag_ready, 1)
            ok = act.value_load(flag[0:1, 0:1], min_val=0, max_val=P)
            with act.If(ok < P):
                attend(second)
                act.wait_ge(second.exp_done, EXP_0 + 2 * (HEADS * STEPS + LAG))
                act.sem_inc(pass2_end, 1)
                act.wait_ge(pass2_end, 3)

            with act.Fori(0, NT // 4) as g:
                for b in range(2):
                    act.wait_ge(c_turned, g + 2)
                    act.activation(ctxT[:, b, :], banks[:, b, :], ACT.Copy).then_inc(cT_ready, 1)

        @block.vector
        def _(dve):
            links = [0]

            def link(ins):
                links[0] += 1
                ins.then_inc(ln_chain, 1)
                dve.wait_ge(ln_chain, links[0])

            def make_scale(i):
                g, r, s, inv = (fscale[:, i, j:j + 1] for j in range(4))
                link(dve.tensor_scalar(g, amax_all[:, i:i + 1], 1e-12, None, ALU.max))
                link(dve.reciprocal(r, g))
                link(dve.tensor_scalar(s, r, FP8_MAX, FP8_MAX, ALU.mult, ALU.min))
                link(dve.reciprocal(inv, s))

            def quantise(dst, src, s, step):
                y, c, r = (t[:, :] for t in qt)
                step(dve.tensor_scalar(y, src, s, None, ALU.mult))
                step(dve.tensor_scalar(c.bitcast(I32), y.bitcast(I32), EXPONENT_BITS, None, ALU.bitwise_and))
                step(dve.tensor_scalar(c, c, FP8_MIN_NORMAL, ROUND_TO_3_BITS, ALU.max, ALU.mult))
                step(dve.tensor_tensor(r, y, c, ALU.add))
                step(dve.tensor_tensor(y, r, c, ALU.subtract))
                return dve.tensor_scalar(dst, y, FP8_MAX, -FP8_MAX, ALU.min, ALU.max)

            dve.wait_ge(w_in["f"], 16)
            wf_flat = w_sb["f"][:, :, :].rearrange("p k n -> p (k n)")
            dve.tensor_reduce(amax[:, 1, 0:1], wf_flat, AX.X, ALU.max, apply_absolute_value=True
                              ).then_inc(amax_ready, 1)
            for g in range(4):
                dve.wait_ge(x_in[g], 16)
                cols = slice(8 * g, 8 * g + 8)
                for i in range(8):
                    last = dve.bn_stats(stats[:, i, :], x_all[:, 8 * g + i, :])
                link(last)
                for i in range(8):
                    last = dve.bn_aggr(mean_var[:, 8 * g + i, :], stats[:, i, :])
                link(last)
                dve.tensor_scalar(ln[:, 0, cols], mean_var[:, cols, 1], EPS, None, ALU.add).then_inc(var_ready, 1)
                dve.wait_ge(root_ready, g + 1)
                link(dve.reciprocal(ln[:, 2, cols], ln[:, 1, cols]))
                link(dve.tensor_tensor(ln[:, 3, cols], ln[:, 2, cols], ln[:, 2, cols], ALU.mult))
                link(dve.tensor_tensor(ln[:, 3, cols], ln[:, 3, cols], ln[:, 0, cols], ALU.mult))
                link(dve.tensor_scalar(ln[:, 3, cols], ln[:, 3, cols], -0.5, 1.5, ALU.mult, ALU.add))
                link(dve.tensor_tensor(ln[:, 4, cols], ln[:, 2, cols], ln[:, 3, cols], ALU.mult))
                for i in range(8 * g, 8 * g + 8):
                    last = dve.tensor_scalar(xn_all[:, i, :], x_all[:, i, :], mean_var[:, i, 0:1], ln[:, 4, i:i + 1],
                                             ALU.subtract, ALU.mult)
                last.then_inc(xn_ready, 1)
                dve.wait_ge(xn_ready, g + 1)
                last = dve.tensor_reduce(amax[:, 0, g:g + 1], xn_all[:, cols, :], AX.XY, ALU.max,
                                         apply_absolute_value=True)
                link(last)
            dve.tensor_reduce(amax[:, 0, 7:8], amax[:, 0, 0:4], AX.X, ALU.max).then_inc(amax_ready, 1)
            dve.wait_ge(amax_shared, 1)
            make_scale(1)
            link(quantise(w8T[:, :, :].rearrange("p k n -> p (k n)"), wf_flat, fscale[:, 1, 2:3], link))

            with dve.Fori(0, NCH // 2) as cc:
                for par in range(2):
                    n = cc * 2 + par

                    def remainder(o):
                        half, which = divmod(o, 2)
                        dve.wait_ge(lo_done, n * 4 + (LO_0 + o - 1))
                        dve.wait_ge(hi_done, n * 4 + (o + 1))
                        dve.scalar_tensor_tensor(out=rest[o % 2][:, :], in0=banks[:, 2 + o, :],
                                                 scalar=qk_bias[:, which, half:half + 1], in1=parts[o][:, 0, :],
                                                 op0=ALU.add, op1=ALU.subtract).then_inc(rest_done, 1)

                    def low(o):
                        dve.wait_ge(mid_done, n * 4 + (o + 1))
                        dve.tensor_tensor(parts[o][:, 2, :], rest[o % 2][:, :], parts[o][:, 1, :],
                                          ALU.subtract).then_inc(lo_done, 1)

                    remainder(0)
                    remainder(1)
                    low(0)
                    remainder(2)
                    low(1)
                    remainder(3)
                    low(2)
                    low(3)
                    for b in range(2):
                        dve.wait_ge(v_mm, n * 2 + (b + 1))
                        dve.tensor_tensor(v_all[:, bass.ds(n * CT + 2 * b, 2), :],
                                          banks[:, 6 + b, :].rearrange("p (t d) -> p t d", t=2), bv_sb[:, :, :],
                                          ALU.add).then_inc(v_done, 1)
            dve.wait_ge(amax_shared, 2)
            make_scale(0)
            link(dve.tensor_tensor(out_scale[:, :], fscale[:, 0, 3:4], fscale[:, 1, 3:4], ALU.mult))

            QUANT_STEPS = 6
            qn = [0]

            def attend(c):
                MAX_LINKS = 3 + c.full * UT
                SUM_LINKS = 1 if c.full else 2
                HEAD_LINKS = 2 * (MAX_LINKS + SUM_LINKS)

                def chain(ins, count):
                    ins.then_inc(c.chain, 1)
                    dve.wait_ge(c.chain, count)

                def maxima(job0, link0):
                    if c.full:
                        with dve.Fori(0, UT) as i:
                            for kb in range(S // CHUNK):
                                dve.wait_ge(c.misc_full, i * (S // CHUNK) + (job0 + kb + 1))
                                dve.tensor_reduce(mpart[:, kb:kb + 1], misc, AX.X, ALU.max).then_inc(c.misc_free, 1)
                            dve.wait_ge(c.misc_free, i * (S // CHUNK) + (job0 + S // CHUNK))
                            chain(dve.tensor_reduce(mcol[:, bass.ds(i, 1)], mpart[:, :], AX.X, ALU.max),
                                  i + (link0 + 1))
                        link0 = link0 + UT
                    else:
                        for j in range(c.max_jobs):
                            dve.wait_ge(c.misc_full, job0 + (j + 1))
                            dve.tensor_reduce(mcol[:, 4 * j:4 * j + 4], misc.rearrange("p (t k) -> p t k", t=4),
                                              AX.X, ALU.max).then_inc(c.misc_free, 1)
                        dve.wait_ge(c.misc_free, job0 + c.max_jobs)
                    chain(dve.tensor_scalar(neg[:, 0, :], mcol[:, :], -1.0, None, ALU.mult), link0 + 1)
                    chain(dve.scalar_tensor_tensor(out=neg_rest[:, :], in0=mcol[:, :], scalar=-1.0, in1=neg[:, 0, :],
                                                   op0=ALU.mult, op1=ALU.subtract), link0 + 2)
                    chain(dve.tensor_copy(neg[:, 1, :], neg_rest[:, :]), link0 + 3)
                    dve.tensor_tensor(neg[:, 2, :], neg_rest[:, :], neg[:, 1, :], ALU.subtract).then_inc(c.neg_ready, 1)
                    job = job0 + c.max_jobs
                    dve.wait_ge(c.misc_full, job + 1)
                    dve.tensor_copy(neg_row[:, :], misc.bitcast(BF16)[0:PARTS * UT, 0:P]
                                    ).then_inc(c.row_ready, 1)
                    dve.wait_ge(c.row_ready, neg_count[0])
                    dve.sem_inc(c.misc_free, 1)

                neg_count = [1]

                def take_sums(h, u, link0):
                    dve.wait_ge(c.pv_done, h * STEPS + (PV_0 + (u + 1) * KT))
                    dve.tensor_copy(o_sb[:, :], acc).then_inc(c.acc_free, 1)
                    dve.wait_ge(c.acc_free, h * 2 + (u + 1 + ACC_0))
                    if not c.full:
                        chain(dve.tensor_scalar(o_junk[:, :], o_sb[:, :], 0.0, None, ALU.mult, ALU.add,
                                                accum_out=o_inf[:, bass.ds(h * 2 + u, 1)]), link0 + 1)

                def normalise(h, u, job, link0):
                    sums = misc.rearrange("p (c j d) -> p c j d", c=4, j=QB)
                    dve.wait_ge(c.misc_full, job + 1)
                    chain(dve.reciprocal(rden[:, :].rearrange("p (c j) -> p c j", c=4), sums[:, :, :, DH]), link0 + 1)
                    for cc in range(4):
                        dst = ctx_all[:, u * UT:(u + 1) * UT, bass.ds(h * DH, DH)]
                        last = dve.tensor_tensor(
                            dst.rearrange("p (j c) d -> p c j d", c=4)[:, cc], sums[:, cc, :, 0:DH],
                            rden[:, QB * cc:QB * (cc + 1)].unsqueeze(2).to_broadcast([P, QB, DH]), ALU.mult)
                    last.then_inc(c.misc_free, 1)

                maxima(0, 0)
                JOB0 = c.max_jobs + 1
                with dve.Fori(0, HEADS) as h:
                    job = h * c.head_jobs + JOB0
                    lk = h * HEAD_LINKS + MAX_LINKS
                    neg_count[0] = h * 2 + 2
                    maxima(job, lk)
                    take_sums(h, 0, lk + MAX_LINKS)
                    normalise(h, 0, job + (c.max_jobs + 1), lk + (MAX_LINKS + SUM_LINKS - 1))
                    if not c.full:
                        dve.wait_ge(xq_in, h * 16 + 16)
                        qn[0] = 0

                        def qstep(ins):
                            qn[0] += 1
                            ins.then_inc(quant_chain, 1)
                            dve.wait_ge(quant_chain, h * QUANT_STEPS + qn[0])

                        quantise(x8T[:, :, :].rearrange("p k s -> p (k s)")[:, bass.ds(h * CHUNK, CHUNK)], xq,
                                 fscale[:, 0, 2:3], qstep).then_inc(xq_used, 1)
                        two = x_all[:, bass.ds(h * 2, 2), :]
                        qstep(dve.tensor_tensor(two, two, bo_sb[:, :, :], ALU.add))
                    neg_count[0] = h * 2 + 3
                    lk = lk + (MAX_LINKS + SUM_LINKS)
                    maxima(job + (c.max_jobs + 2), lk)
                    take_sums(h, 1, lk + MAX_LINKS)
                    normalise(h, 1, job + (2 * c.max_jobs + 3), lk + (MAX_LINKS + SUM_LINKS - 1))

            attend(first)
            link(dve.tensor_reduce(all_ok[:, 0:1], o_inf[:, :], AX.X, ALU.add))
            dve.tensor_scalar(all_ok[:, 1:2], all_ok[:, 0:1], 0.0, None, ALU.is_equal).then_inc(flag_ok, 1)
            dve.wait_ge(flag_sum, 1)
            dve.tensor_copy(flag[0:1, 0:1], misc[0:1, 0:1]).then_inc(flag_ready, 1)
            dve.wait_ge(flag_ready, 1)
            ok = dve.value_load(flag[0:1, 0:1], min_val=0, max_val=P)
            with dve.If(ok < P):
                attend(second)
                dve.wait_ge(second.misc_free, HEADS * second.head_jobs + second.max_jobs + 1)
                dve.sem_inc(pass2_end, 1)
                dve.wait_ge(pass2_end, 3)

            with dve.Fori(0, NT // 4) as g:
                for b in range(2):
                    dve.wait_ge(out_ready, g * 2 + (b + 1))
                    dve.wait_ge(ffn_done, g * 2 + (b + 1))
                    dve.scalar_tensor_tensor(out=y_sb[b], in0=banks[:, 4 + b, :], scalar=out_scale[:, 0:1],
                                             in1=bf_sb[:, :, :].rearrange("p t d -> p (t d)"), op0=ALU.mult,
                                             op1=ALU.add).then_inc(y_done, 1)
                for b in range(2):
                    dve.wait_ge(proj_done, g * 2 + (b + 1))
                    dve.tensor_tensor(res[b][:, :].rearrange("p (t d) -> p t d", t=2),
                                      banks[:, 2 + b, :].rearrange("p (t d) -> p t d", t=2),
                                      x_all[:, bass.ds(g * 4 + 2 * b, 2), :], ALU.add).then_inc(res_done, 1)
                    dve.wait_ge(res_done, g * 2 + (b + 1 + 2))
                    dve.wait_ge(y_done, g * 2 + (2 + 2))
                    dve.wait_ge(out_saved[b], g * 16 + OUT_0)
                    dve.tensor_tensor(o_out[b][:, :], res[b][:, :], y_sb[b], ALU.add).then_inc(out_ready, 1)

        @block.tensor
        def _(pe):
            pe.wait_ge(consts, 8)
            for n in "qkv":
                pe.wait_ge(w_in[n], 16)
            with pe.Fori(0, NCH // 2) as cc:
                for par in range(2):
                    n = cc * 2 + par
                    pe.wait_ge(xnc_ready, n + 1)
                    pe.wait_ge(xT_ready, n * 2 + XT_0)
                    for k in range(KD):
                        for j in range(CT):
                            last = pe.transpose(banks[:, k, j * P:(j + 1) * P], xnc[par][:, j, k * P:(k + 1) * P],
                                                ident[:, :])
                        last.then_inc(turned, 1)
                    pe.wait_ge(xT_ready, n * 2 + (XT_0 + 2))
                    for o in range(4):
                        half, which = divmod(o, 2)
                        pe.wait_ge(rest_done, n * 4 + (REST_0 - 4 + o + 1))
                        for k in range(KD):
                            last = pe.matmul(banks[:, 2 + o, :],
                                             w_sb["qk"[which]][:, k, half * P:(half + 1) * P],
                                             xnTc[par][:, k, :], start=(k == 0), stop=(k == KD - 1))
                        last.then_inc(qk_done, 1)
                    for b in range(2):
                        pe.wait_ge(v_done, n * 2 + (V_0 - 2 + b + 1))
                        for j in range(2):
                            for k in range(KD):
                                t = 2 * b + j
                                last = pe.matmul(banks[:, 6 + b, j * D:(j + 1) * D],
                                                 xnTc[par][:, k, t * P:(t + 1) * P], w_sb["v"][:, k, :],
                                                 start=(k == 0), stop=(k == KD - 1))
                        last.then_inc(v_mm, 1)
            pe.wait_ge(rest_done, REST_0 + 4 * NCH)
            pe.wait_ge(v_done, V_0 + 2 * NCH)
            pe.wait_ge(xT_ready, XT_0 + 2 * NCH)

            def attend(c):
                def misc_job(job, ready):
                    if ready:
                        pe.wait_ge(c.misc_free, job)

                def max_job(u, j, job, ready=True):
                    misc_job(job, ready)
                    for i in range(4):
                        at = u * UQ + (4 * j + i) * P
                        last = pe.matmul(misc[:, i * P:(i + 1) * P], q_st[0:KROWS, at:at + P], k_st[0:KROWS, 0:AK],
                                         start=True, stop=True)
                    last.then_inc(c.misc_full, 1)

                def all_max_jobs(u, job0, loads):
                    with pe.Fori(0, UT) as i:
                        for s in (c.q_in[u], *c.k_in):
                            pe.wait_ge(s, loads)
                        for kb in range(S // CHUNK):
                            pe.wait_ge(c.misc_free, i * (S // CHUNK) + (job0 + kb))
                            pe.matmul(misc, q_st[0:KROWS, bass.ds(i * P + u * UQ, P)],
                                      k_st[0:KROWS, kb * CHUNK:(kb + 1) * CHUNK], start=True, stop=True
                                      ).then_inc(c.misc_full, 1)

                def turn_maxima(job, count):
                    misc_job(job, True)
                    pe.wait_ge(c.neg_ready, count)
                    pe.transpose(misc.bitcast(BF16)[:, 0:P], neg[:, :, :].rearrange("p a t -> p (a t)"),
                                 ident_bf[:, :]).then_inc(c.misc_full, 1)

                def turn_sums(h, u, job):
                    misc_job(job, True)
                    pe.wait_ge(c.acc_free, h * 2 + (u + 1 + ACC_0))
                    for i in range(4):
                        last = pe.transpose(misc[:, i * P:(i + 1) * P], o_sb[:, i * P:(i + 1) * P], ident[:, :])
                    last.then_inc(c.misc_full, 1)

                def scores(h, t):
                    base = 2 * t
                    tt = t % STEPS
                    u, kt = divmod(tt, KT)
                    if kt == 0:
                        pe.wait_ge(c.row_in[u], h * 48 + 48 * (1 + t // STEPS))
                        pe.wait_ge(c.q_in[u], h * (16 * TERMS) + 16 * TERMS * (1 + t // STEPS))
                    if u == 0 and kt % (KT // 2) == 0:
                        pe.wait_ge(c.k_in[kt // (KT // 2)], h * (16 * TERMS) + 16 * TERMS * (1 + t // STEPS))
                    for a in range(2):
                        i = 2 * tt + a
                        before = {0: 2, 1: 2, 2: 5}.get(i, NB)
                        pe.wait_ge(c.exp_done, h * (2 * STEPS) + (EXP_0 + base + a - before + 1))
                        for j in range(2):
                            qb = 2 * a + j
                            last = pe.matmul(banks[:, 2 * (i % NB) + j, :], k_st[:, kt * P:(kt + 1) * P],
                                             q_st[:, u * UQ + qb * CHUNK:u * UQ + (qb + 1) * CHUNK],
                                             start=True, stop=True)
                        last.then_inc(c.st_done, 1)

                def weighted_sum(h, t):
                    u, kt = divmod(t, KT)
                    if kt == 0:
                        pe.wait_ge(c.acc_free, h * 2 + (u + ACC_0))
                    if u == 0 and kt % (KT // 2) == 0:
                        pe.wait_ge(c.v_in[kt // (KT // 2)], h + 1)
                    pe.wait_ge(c.exp_done, h * (2 * STEPS) + (EXP_0 + 2 * t + 2))
                    for qb in range(QB):
                        last = pe.matmul(banks[VCOLS * qb:VCOLS * (qb + 1), 6, :], v_st[:, kt, :],
                                         probs[:, t % SLOTS, qb * CHUNK:(qb + 1) * CHUNK],
                                         start=(kt == 0), stop=(kt == KT - 1), tile_position=(0, VCOLS * qb))
                    last.then_inc(c.pv_done, 1)

                pe.wait_ge(c.q_in[0], 16 * TERMS)
                pe.wait_ge(c.k_in[0], 16 * TERMS)
                if c.full:
                    pe.wait_ge(c.k_in[1], 16 * TERMS)
                    pe.wait_ge(flag_ready, 1)
                    with pe.Fori(0, UT) as i:
                        for kb in range(S // CHUNK):
                            if kb:
                                pe.wait_ge(c.misc_free, i * (S // CHUNK) + kb)
                            pe.matmul(misc, q_st[0:KROWS, bass.ds(i * P, P)],
                                      k_st[0:KROWS, kb * CHUNK:(kb + 1) * CHUNK], start=True, stop=True
                                      ).then_inc(c.misc_full, 1)
                            if kb == S // CHUNK - 1:
                                pe.wait_ge(c.misc_free, i * (S // CHUNK) + (kb + 1))
                else:
                    for j in range(c.max_jobs):
                        max_job(0, j, j, ready=j > 0)
                turn_maxima(c.max_jobs, 1)
                JOB0 = c.max_jobs + 1
                for t in range(LAG):
                    scores(0, t)

                with pe.Fori(0, HEADS) as h:
                    job = h * c.head_jobs + JOB0
                    early = {}
                    if not c.full:
                        for j, t in enumerate((14, 16, 18, 20)):
                            early[t] = (1, j, job + j)
                        for j, t in enumerate((51, 52, 53, 54)):
                            early[t] = (0, j, job + (c.max_jobs + 2 + j))
                    for t in range(STEPS):
                        weighted_sum(h, t)
                        if c.full and (t + LAG) % KT == 0:
                            u = (t + LAG) // KT % 2
                            nxt = (t + LAG) // STEPS
                            j0 = job if u else job + (c.max_jobs + 2)
                            all_max_jobs(u, j0, h * (16 * TERMS) + 16 * TERMS * (1 + nxt))
                            turn_maxima(j0 + c.max_jobs, h * 2 + (2 if u else 3))
                        if t in early:
                            u, j, jb = early[t]
                            if j == 0:
                                pe.wait_ge(c.q_in[u], h * (16 * TERMS) + 16 * TERMS * (2 - u))
                                pe.wait_ge(c.k_in[0], h * (16 * TERMS) + 16 * TERMS * (2 - u))
                            max_job(u, j, jb)
                        if not c.full and t == 22:
                            turn_maxima(job + c.max_jobs, h * 2 + 2)
                        if not c.full and t == 57:
                            turn_maxima(job + (2 * c.max_jobs + 2), h * 2 + 3)
                        scores(h, t + LAG)
                        if t == KT + 1:
                            turn_sums(h, 0, job + (c.max_jobs + 1))
                    turn_sums(h, 1, job + (2 * c.max_jobs + 3))
                pe.wait_ge(c.exp_done, EXP_0 + 2 * (HEADS * STEPS + LAG))

            attend(first)
            pe.wait_ge(first.misc_free, HEADS * first.head_jobs + first.max_jobs + 1)
            pe.wait_ge(flag_ok, 1)
            pe.matmul(misc[0:1, 0:1], all_ok[:, 1:2], ones[:, :], start=True, stop=True).then_inc(flag_sum, 1)
            pe.wait_ge(flag_ready, 1)
            ok = pe.value_load(flag[0:1, 0:1], min_val=0, max_val=P)
            with pe.If(ok < P):
                attend(second)
                pe.wait_ge(second.misc_free, HEADS * second.head_jobs + second.max_jobs + 1)
                pe.sem_inc(pass2_end, 1)
                pe.wait_ge(pass2_end, 3)

            pe.wait_ge(w_in["o"], 16)
            with pe.Fori(0, NT // 4) as g:
                pe.wait_ge(cx_ready, g + 1)
                for b in range(2):
                    for j in range(2):
                        for k in range(KD):
                            last = pe.transpose(banks[:, b, (2 * k + j) * P:(2 * k + j + 1) * P],
                                                cx[:, 2 * b + j, k * P:(k + 1) * P], ident[:, :])
                last.then_inc(c_turned, 1)
                for b in range(2):
                    pe.wait_ge(y_done, g * 2 + (b + 1))
                    for j in range(2):
                        for k in range(KD):
                            last = pe.matmul(banks[:, 4 + b, j * D:(j + 1) * D],
                                             x8T[:, k, bass.ds(g * (4 * P) + (2 * b + j) * P, P)], w8T[:, k, :],
                                             start=(k == 0), stop=(k == KD - 1))
                    last.then_inc(ffn_done, 1)
                for b in range(2):
                    pe.wait_ge(cT_ready, g * 2 + (b + 1))
                    pe.wait_ge(res_done, g * 2 + (b + 1))
                    for j in range(2):
                        for k in range(KD):
                            last = pe.matmul(banks[:, 2 + b, j * D:(j + 1) * D],
                                             ctxT[:, b, (2 * k + j) * P:(2 * k + j + 1) * P], w_sb["o"][:, k, :],
                                             start=(k == 0), stop=(k == KD - 1))
                    last.then_inc(proj_done, 1)


_INS = ["L0_attn_query", "L0_attn_q_w", "L0_attn_q_b", "L0_attn_k_w", "L0_attn_k_b", "L0_attn_v_w", "L0_attn_v_b",
        "L0_attn_out_w", "L0_attn_out_b", "L0_ffn_weight", "L0_ffn_bias"]


def kernel(**inputs):
    import numpy as _np
    import concourse.bacc as _bacc
    from concourse import mybir as _mybir
    from concourse.bass_utils import run_bass_kernel_spmd as _run

    nc = _bacc.Bacc("TRN2", target_bir_lowering=False, num_devices=1)
    arrays, args = {}, []
    for name in _INS:
        a = _np.asarray(inputs[name])
        if name.endswith("_w") or name.endswith("weight"):
            a = a.T
        a = _np.ascontiguousarray(a)
        arrays[f"in_{name}_dram"] = a
        args.append(nc.dram_tensor(f"in_{name}_dram", a.shape, _mybir.dt.from_np(a.dtype), kind="ExternalInput").ap())
    shape = inputs["L0_attn_query"].shape
    args.append(nc.dram_tensor("out_0_dram", shape, _mybir.dt.float32, kind="ExternalOutput").ap())
    program(nc, *args)
    r = _run(nc, [arrays], core_ids=[0])
    return r.results[0]["out_0_dram"]
```

```python
from contextlib import ExitStack

import concourse.bass as bass
from concourse import mybir

ALU = mybir.AluOpType
ACT = mybir.ActivationFunctionType
AX = mybir.AxisListType
F32 = mybir.dt.float32
BF16 = mybir.dt.bfloat16
I32 = mybir.dt.int32

P = 128
HEADS = 16
EPS = 1e-5
FP8_MAX = 448.0
FP8_MIN_NORMAL = 2.0 ** -6
ROUND_TO_3_BITS = 1.5 * 2.0 ** 20
EXPONENT_BITS = 0x7F800000
PARTS = 3
TERMS = 6
OVERFLOW_MARGIN = 2.0 ** 10
HEADROOM = 16.0
LEAD = 3
WIDE = 2
BUFS = 3
RING = 16
VCOLS = 32


def program(nc, x, wq, bq, wk, bk, wv, bv, wo, bo, wf, bf, out):
    _, S, D = x.shape
    DH = D // HEADS
    KD = D // P
    NT = S // P
    CHUNK = 512
    CT = CHUNK // P
    NCH = S // CHUNK
    QB = 4
    UQ = QB * CHUNK
    UNITS = S // UQ
    KT = S // P
    STEPS = UNITS * KT
    UT = UQ // P
    KROWS = TERMS * DH
    STACK = KROWS + PARTS
    UT4 = QB * KT
    UE = -(-UT4 // WIDE)
    HT, HE = UNITS * UT4, UNITS * UE
    AK = 64
    JT = CHUNK // AK
    SCALE = float(DH) ** -0.5
    NH1 = HEADS + 1
    assert (KD, UNITS, DH, TERMS * DH, RING % WIDE) == (2, 2, 16, 96, 0)

    q_dram = nc.dram_tensor("q_parts", [PARTS, NH1 * DH, S], BF16, kind="Internal").ap()
    k_dram = nc.dram_tensor("k_parts", [PARTS, NH1 * DH, S], BF16, kind="Internal").ap()
    xnT_dram = nc.dram_tensor("xnT_copy", [P, KD, S], F32, kind="Internal").ap()

    with ExitStack() as ctx:
        def sb(name, shape, dt=F32):
            return ctx.enter_context(nc.sbuf_tensor(name, shape, dt))

        def sem(name):
            return ctx.enter_context(nc.semaphore(name))

        x_all = sb("x_all", [P, NT, D])
        xn_all = sb("xn_all", [P, NT, D])
        ctx_all = xn_all
        v_all = sb("v_all", [P, NT, D])
        w_sb = {n: sb(f"w_{n}", [P, KD, D]) for n in "qkvof"}
        qk_bias = sb("qk_bias", [P, 2, KD])
        bv_sb = sb("bv_sb", [P, 2, D])
        bo_sb = sb("bo_sb", [P, 2, D])
        bf_sb = sb("bf_sb", [P, 2, D])
        ident = sb("ident", [P, P])
        ident_bf = sb("ident_bf", [P, P], BF16)
        ones = sb("ones", [P, 1])
        zeros = sb("zeros", [P, 1])
        table_pad = sb("table_pad", [P, 1])
        stats = sb("stats", [P, 8, 6])
        ln = sb("ln", [P, 6, 8])
        amax = sb("amax", [P, 2, 8])
        amax_all = sb("amax_all", [P, 2])
        fscale = sb("fscale", [P, 2, 4])
        out_scale = sb("out_scale", [P, 1])
        parts = [sb(f"parts{i}", [P, PARTS, CHUNK], BF16) for i in range(4)]
        q_st = sb("q_st", [STACK, S], BF16)
        k_st = sb("k_st", [STACK, S], BF16)
        v_st = sb("v_st", [P, KT, VCOLS])
        probs = sb("probs", [P, RING * CHUNK])
        xnc = [probs[:, i * CT * D:(i + 1) * CT * D].rearrange("p (t d) -> p t d", t=CT) for i in range(2)]
        xnTc = [probs[:, (2 + i) * CT * D:(3 + i) * CT * D].rearrange("p (k c) -> p k c", k=KD) for i in range(2)]
        xnT_again = [probs[:, i * CT * D:(i + 1) * CT * D].rearrange("p (k c) -> p k c", k=KD) for i in range(4)]
        mcol = sb("mcol", [P, UT])
        mpart = sb("mpart", [P, S // CHUNK])
        neg = sb("neg", [P, P // UT, UT], BF16)
        neg_full = sb("neg_full", [P, UT])
        neg_rest = sb("neg_rest", [P, UT])
        neg_row = sb("neg_row", [PARTS * UT, P], BF16)
        o_sb = sb("o_sb", [P, CHUNK])
        o_junk = sb("o_junk", [P, CHUNK])
        o_inf = sb("o_inf", [P, UNITS * HEADS])
        rden = sb("rden", [P, UT])
        all_ok = sb("all_ok", [P, 2])
        flag = sb("flag", [1, 1], I32)
        rest = [o_sb, o_junk]
        xq = w_sb["f"][:, :, :].rearrange("p k n -> p (k n)")
        qt = [sb("qt0", [P, CHUNK]), sb("qt1", [P, CHUNK]), o_junk]
        x8T = sb("x8T", [P, KD, S], BF16)
        w8T = sb("w8T", [P, KD, D], BF16)
        cx = xnc[0]
        ctxT = xnTc[0]
        y_sb = [parts[i][:, 0, :] for i in range(2)]
        res = rest
        o_out = [qt[0], qt[1]]

        banks = ctx.enter_context(nc.psum_tensor("banks", [P, 8, CHUNK], F32))
        acc = banks[:, 6, :]
        misc = banks[:, 7, :]

        x_in = [sem("x_in_first"), sem("x_in_rest")]
        w_in = {n: sem(f"w_in_{n}") for n in "qkvof"}
        bias_in = sem("bias_in")
        consts = sem("consts")
        ln_chain = sem("ln_chain")
        var_ready = sem("var_ready")
        root_ready = sem("root_ready")
        xn_first = sem("xn_first")
        xn_ready = sem("xn_ready")
        amax_ready = sem("amax_ready")
        amax_shared = sem("amax_shared")
        xnc_ready = sem("xnc_ready")
        turned = sem("turned")
        xT_ready = sem("xT_ready")
        xT_saved = [sem(f"xT_saved{i}") for i in range(2)]
        xT_back = [sem(f"xT_back{i}") for i in range(4)]
        qk_done = sem("qk_done")
        hi_done = sem("hi_done")
        rest_done = sem("rest_done")
        mid_done = sem("mid_done")
        lo_done = sem("lo_done")
        parts_saved = [sem(f"parts_saved{i}") for i in range(4)]
        v_mm = sem("v_mm")
        v_done = sem("v_done")
        flag_ok = sem("flag_ok")
        flag_sum = sem("flag_sum")
        flag_ready = sem("flag_ready")
        pass2_end = sem("pass2_end")
        cx_ready = sem("cx_ready")
        c_turned = sem("c_turned")
        cT_ready = sem("cT_ready")
        ffn_done = sem("ffn_done")
        proj_done = sem("proj_done")
        y_done = sem("y_done")
        res_done = sem("res_done")
        out_ready = sem("out_ready")
        out_saved = [sem(f"out_saved{i}") for i in range(2)]
        xq_in = sem("xq_in")
        xq_used = sem("xq_used")
        quant_chain = sem("quant_chain")

        class Pass:

            def __init__(self, tag, full):
                self.full = full
                self.q_in = [sem(f"{tag}_q_in{i}") for i in range(2)]
                self.k_in = [sem(f"{tag}_k_in{i}") for i in range(2)]
                self.row_in = [sem(f"{tag}_row_in{i}") for i in range(2)]
                self.v_in = [sem(f"{tag}_v_in{i}") for i in range(2)]
                self.st_done = sem(f"{tag}_st_done")
                self.exp_done = sem(f"{tag}_exp_done")
                self.pv_done = sem(f"{tag}_pv_done")
                self.acc_free = sem(f"{tag}_acc_free")
                self.misc_full = sem(f"{tag}_misc_full")
                self.misc_free = sem(f"{tag}_misc_free")
                self.neg_ready = sem(f"{tag}_neg_ready")
                self.row_ready = sem(f"{tag}_row_ready")
                self.chain = sem(f"{tag}_chain")
                self.max_jobs = UT * (S // CHUNK) if full else UT // JT
                self.head_jobs = 2 * (self.max_jobs + 1)

        first = Pass("a", False)
        second = Pass("b", True)

        REST_0, LO_0, SAVED_0, V_0 = 4, 4, 16, 4
        SAVES = 32 * 4 + 16 * 4
        EXP_0 = 2 * HE
        PV_0 = STEPS
        ACC_0 = 1
        OUT_0 = 16

        FIRST_MAX = {3: 0, 4: 1}
        TURN_FIRST = 5

        def term(o, par):
            return 2 + 2 * par + o, parts[2 * par + o]

        def saved_before(cc, second_half):
            if second_half:
                return cc * 16 + (SAVED_0 + 32 * 4)
            return cc * 32 + SAVED_0

        def exp_of(tile):
            u, r = divmod(tile, UT4)
            return u * UE + r // WIDE, r % WIDE, min(WIDE, UT4 - r // WIDE * WIDE)

        def banks_user(e):
            return BUFS if e >= BUFS else e + HE - ((HE - 1 - e) // BUFS * BUFS + e)

        def ring_user(tile):
            u, r = divmod(tile, UT4)
            r -= RING
            if r < 0:
                u, r = u - 1, r + RING
                r += (UT4 - 1 - r) // RING * RING
            return u * KT + r // QB

        tok = "(t p) d -> p t d"
        x_v = x.rearrange("b s d -> (b s) d").rearrange(tok, p=P)
        out_v = out.rearrange("b s d -> (b s) d").rearrange(tok, p=P)

        block = ctx.enter_context(nc.Block())

        @block.sync
        def _(sp):
            wn = {"q": wq, "k": wk, "v": wv, "o": wo, "f": wf}

            def load_w(n):
                sp.dma_start(w_sb[n][:, :, :], wn[n].rearrange("(k p) n -> p k n", p=P)).then_inc(w_in[n], 16)

            def load_x(t0, t1, s):
                sp.dma_start(x_all[:, t0:t1, :], x_v[:, t0:t1, :]).then_inc(s, 16)

            for t in range(0, 8, 2):
                load_x(t, t + 2, x_in[0])
            load_w("q")
            load_w("k")
            load_x(8, 16, x_in[1])
            load_w("v")
            for i, b in enumerate((bq, bk)):
                sp.dma_start(qk_bias[:, i, :], b.rearrange("(k p) -> p k", p=P),
                             allow_slow_non_contiguous=True).then_inc(bias_in, 16)
            for i in range(2):
                sp.dma_start(bv_sb[:, i, :], bv.partition_broadcast(P)).then_inc(bias_in, 16)
            load_x(16, 24, x_in[1])
            load_x(24, 32, x_in[1])
            load_w("f")
            load_w("o")
            for t, b in ((bo_sb, bo), (bf_sb, bf)):
                for i in range(2):
                    sp.dma_start(t[:, i, :], b.partition_broadcast(P)).then_inc(bias_in, 16)

            for s, n in ((rest_done, REST_0), (lo_done, LO_0), (v_done, V_0),
                         (y_done, 2), (res_done, 2), (out_ready, 2),
                         (out_saved[0], OUT_0), (out_saved[1], OUT_0), (c_turned, 1),
                         (xT_saved[0], SAVED_0), (xT_saved[1], SAVED_0)):
                sp.sem_inc(s, n)
            for i in range(4):
                sp.sem_inc(parts_saved[i], SAVED_0)
            for c in (first, second):
                sp.sem_inc(c.exp_done, EXP_0)
                sp.sem_inc(c.pv_done, PV_0)
                sp.sem_inc(c.acc_free, ACC_0)

            def save_parts(n, cc, par, half):
                cols = bass.ds(cc * CHUNK + par * UQ, CHUNK)
                for o in range(2):
                    if o or half:
                        sp.wait_ge(lo_done, n * 2 + (LO_0 + o + 1 + half * 2 * NCH))
                    buf, saved = parts[2 * par + o], parts_saved[2 * par + o]
                    dram = (q_dram, k_dram)[o][:, :, cols].rearrange("a r c -> r a c")
                    sp.dma_start(dram[half * P:(half + 1) * P], buf[:, :, :]).then_inc(saved, 16)
                    if half == 0:
                        sp.dma_start(dram[HEADS * DH:NH1 * DH], buf[0:DH, :, :]).then_inc(saved, 16)

            def save_chunk(cc, par):
                n = cc * 2 + par
                sp.wait_ge(lo_done, n * 2 + (LO_0 + 1))
                sp.dma_start(xnT_dram[:, :, bass.ds(n * CHUNK, CHUNK)], xnTc[par][:, :, :]
                             ).then_inc(xT_saved[par], 16)
                save_parts(n, cc, par, 0)

            with sp.Fori(0, NCH // 2 - 1) as cc:
                for par in range(2):
                    save_chunk(cc, par)

            def load_xT(n):
                sp.dma_start(xnT_again[n % 4][:, :, :], xnT_dram[:, :, n * CHUNK:(n + 1) * CHUNK]
                             ).then_inc(xT_back[n % 4], 16)

            for n in range(2):
                sp.wait_ge(turned, 2 * (NCH - 1 + n))
                sp.wait_ge(xT_saved[n], SAVED_0 + 16)
                load_xT(n)
                save_chunk(NCH // 2 - 1, n)
            for n in range(2, 4):
                sp.wait_ge(v_mm, 2 * (NCH - 1 + n - 2))
                sp.wait_ge(xT_saved[n % 2], SAVED_0 + 16 * (NCH // 2))
                load_xT(n)
            for i in range(4):
                sp.wait_ge(parts_saved[i], SAVED_0 + 32 * 4)

            def load_q(c, head, u):
                rows, cols = bass.ds(head * DH, DH), slice(u * UQ, (u + 1) * UQ)
                at = 0
                for a in (3, 2, 1):
                    for i in range(a):
                        sp.dma_start(q_st[at:at + DH, cols], q_dram[i, rows, cols]).then_inc(c.q_in[u], 16)
                        at += DH

            def load_k(c, head, half):
                rows, cols = bass.ds(head * DH, DH), slice(half * (S // 2), (half + 1) * (S // 2))
                for at, i in enumerate((0, 0, 0, 1, 1, 2)):
                    sp.dma_start(k_st[at * DH:(at + 1) * DH, cols], k_dram[i, rows, cols]).then_inc(c.k_in[half], 16)

            def load_rows(c, u, count):
                sp.wait_ge(c.row_ready, count)
                for i in range(PARTS):
                    sp.dma_start(q_st[KROWS + i:KROWS + i + 1, u * UQ:(u + 1) * UQ]
                                 .rearrange("o (t c) -> o t c", c=P),
                                 neg_row[i * UT:(i + 1) * UT, :]).then_inc(c.row_in[u], 16)

            def load_first_head(c):
                for u in range(2):
                    load_k(c, 0, u)
                    load_q(c, 0, u)

            load_k(first, 0, 0)
            for n in range(NCH):
                if n + 4 < NCH:
                    sp.wait_ge(qk_done, 2 * (NCH + n + 1))
                    load_xT(n + 4)
                if n == TURN_FIRST:
                    load_rows(first, 0, 1)
                save_parts(n, n // 2, n % 2, 1)
                if n == 0:
                    load_q(first, 0, 0)
                elif n == 1:
                    load_k(first, 0, 1)
                elif n == 2:
                    load_q(first, 0, 1)
            for i in range(4):
                sp.wait_ge(parts_saved[i], SAVED_0 + SAVES)

            def attend(c):
                if c.full:
                    load_first_head(c)
                    load_rows(c, 0, 1)
                with sp.Fori(0, HEADS) as h:
                    nxt = sp.snap(h + 1)
                    if not c.full:
                        sp.wait_ge(xq_used, h + 1)
                        half_cols = xnT_dram.rearrange("p k s -> p (k s)")
                        sp.dma_start(xq, half_cols[:, bass.ds(h * CHUNK, CHUNK)]).then_inc(xq_in, 16)
                    load_rows(c, 1, h * 2 + 2)
                    sp.wait_ge(c.st_done, h * HE + UE)
                    load_q(c, nxt, 0)
                    sp.wait_ge(c.st_done, h * HE + (exp_of(UT4 + UT4 // 2 - 1)[0] + 1))
                    load_k(c, nxt, 0)
                    if not c.full:
                        load_rows(c, 0, h * 2 + 3)
                    sp.wait_ge(c.st_done, h * HE + HE)
                    load_k(c, nxt, 1)
                    load_q(c, nxt, 1)
                    if c.full:
                        load_rows(c, 0, h * 2 + 3)
                for u in range(2):
                    sp.wait_ge(c.q_in[u], 16 * TERMS * NH1)
                    sp.wait_ge(c.k_in[u], 16 * TERMS * NH1)

            attend(first)
            sp.wait_ge(flag_ready, 1)
            ok = sp.value_load(flag[0:1, 0:1], min_val=0, max_val=P)
            with sp.If(ok < P):
                attend(second)
                sp.wait_ge(pass2_end, 3)

            with sp.Fori(0, NT // 4) as g:
                for b in range(2):
                    sp.wait_ge(out_ready, g * 2 + (b + 1 + 2))
                    sp.dma_start(out_v[:, bass.ds(g * 4 + 2 * b, 2), :],
                                 o_out[b][:, :].rearrange("p (t d) -> p t d", t=2)).then_inc(out_saved[b], 16)
            for b in range(2):
                sp.wait_ge(out_saved[b], OUT_0 + 16 * (NT // 4))

        @block.gpsimd
        def _(pool):
            count = [0]

            def constant(ins):
                count[0] += 1
                ins.then_inc(consts, 1)
                pool.wait_ge(consts, count[0])

            constant(pool.memset(ident[:, :], 0.0))
            constant(pool.affine_select(out=ident[:, :], in_=ident[:, :], compare_op=ALU.not_equal, fill=1.0, base=0,
                                        pattern=[[-1, P]], channel_multiplier=1))
            constant(pool.tensor_copy(ident_bf[:, :], ident[:, :]))
            constant(pool.memset(v_st[:, :, :], 0.0))
            constant(pool.memset(v_st[:, :, DH:DH + 1], 1.0))
            constant(pool.memset(k_st[KROWS:STACK, :], 1.0))
            constant(pool.memset(ones[:, :], 1.0))
            constant(pool.memset(zeros[:, :], 0.0))
            constant(pool.memset(neg[:, :, :], 0.0))

            def stage_chunk(n, par):
                pool.tensor_copy(xnc[par][:, :, :], xn_all[:, bass.ds(n * CT, CT), :]).then_inc(xnc_ready, 1)

            def low(n, par):
                for o in range(2):
                    pool.wait_ge(mid_done, n * 2 + (o + 1))
                    buf = term(o, par)[1]
                    pool.tensor_tensor(buf[:, 2, :], rest[o][:, :], buf[:, 1, :], ALU.subtract).then_inc(lo_done, 1)

            pool.wait_ge(xn_ready, 1)
            stage_chunk(1, 1)
            with pool.Fori(0, NCH // 2 - 1) as cc:
                for par in range(2):
                    n = cc * 2 + par
                    pool.wait_ge(turned, n * 2 + 2)
                    pool.wait_ge(xn_ready, cc + 2)
                    stage_chunk(n + 2, par)
                    low(n, par)
            for par in range(2):
                low(NCH - 2 + par, par)
            RMAX = bass.bass_isa.ReduceOp.max
            with pool.Fori(0, NCH // 2) as cc:
                for par in range(2):
                    low(cc * 2 + (NCH + par), par)
            pool.wait_ge(amax_ready, 1)
            pool.partition_all_reduce(amax_all[:, :], amax[:, :, 7], P, RMAX).then_inc(amax_shared, 1)
            pool.wait_ge(v_done, V_0 + 2 * NCH)

            def attend(c):
                with pool.Fori(0, HEADS) as h:
                    for half in range(2):
                        pool.wait_ge(c.pv_done, h * STEPS + (PV_0 - STEPS) + KT + (half + 1) * (KT // 2))
                        rows = slice(half * (KT // 2), (half + 1) * (KT // 2))
                        src = v_all.rearrange("p (c u i) d -> p u c i d", u=UNITS, i=CT)[:, half]
                        pool.tensor_copy(v_st[:, rows, 0:DH].rearrange("p (c i) d -> p c i d", i=CT),
                                         src[:, :, :, bass.ds(h * DH, DH)]).then_inc(c.v_in[half], 1)

            attend(first)
            pool.wait_ge(flag_ready, 1)
            ok = pool.value_load(flag[0:1, 0:1], min_val=0, max_val=P)
            with pool.If(ok < P):
                attend(second)
                pool.wait_ge(pass2_end, 3)

            with pool.Fori(0, NT // 4) as g:
                pool.wait_ge(c_turned, g + 1)
                pool.tensor_copy(cx[:, :, :], ctx_all[:, bass.ds(g * 4, 4), :]).then_inc(cx_ready, 1)

        @block.scalar
        def _(act):
            def root(g):
                act.wait_ge(var_ready, g + 1)
                act.activation(ln[:, 1, :], ln[:, 0, :], ACT.Sqrt).then_inc(root_ready, 1)

            def copy_turned(n, par, save_count):
                for k in range(KD):
                    act.wait_ge(turned, n * 2 + (k + 1))
                    if k == 0:
                        act.wait_ge(xT_saved[par], save_count)
                    act.activation(xnTc[par][:, k, :], banks[:, k, :], ACT.Copy).then_inc(xT_ready, 1)

            def high(n, cc, par, o, half):
                bank, buf = term(o, par)
                act.wait_ge(parts_saved[2 * par + o], saved_before(cc, half))
                act.wait_ge(qk_done, n * 2 + (o + 1))
                act.activation(buf[:, 0, :], banks[:, bank, :], ACT.Identity,
                               bias=qk_bias[:, o, half:half + 1]).then_inc(hi_done, 1)

            def middle(n, par, o):
                act.wait_ge(rest_done, n * 2 + (REST_0 + o + 1))
                act.activation(term(o, par)[1][:, 1, :], rest[o][:, :], ACT.Copy).then_inc(mid_done, 1)

            root(0)
            copy_turned(0, 0, SAVED_0)
            act.wait_ge(bias_in, 16 * 8)

            def group(cc, last):
                if not last:
                    root(cc + 1)
                for par in range(2):
                    n = cc * 2 + par
                    high(n, cc, par, 0, 0)
                    high(n, cc, par, 1, 0)
                    if not (last and par):
                        copy_turned(n + 1, 1 - par, cc * 16 + (SAVED_0 + 16 * par))
                    middle(n, par, 0)
                    middle(n, par, 1)

            with act.Fori(0, NCH // 2 - 1) as cc:
                group(cc, False)
            group(NCH // 2 - 1, True)
            with act.Fori(0, NCH // 2) as cc:
                for par in range(2):
                    n = cc * 2 + (NCH + par)
                    for o in range(2):
                        high(n, cc, par, o, 1)
                    for o in range(2):
                        middle(n, par, o)

            def attend(c):
                def exps(h, e):
                    tile = e // UE * UT4 + e % UE * WIDE
                    wide = exp_of(tile)[2]
                    at = tile % UT4 % RING * CHUNK
                    act.wait_ge(c.st_done, h * HE + (e + 1))
                    used = max(ring_user(i) for i in range(tile, tile + wide))
                    act.wait_ge(c.pv_done, h * STEPS + (PV_0 + used + 1))
                    bank = WIDE * (e % BUFS)
                    act.activation(probs[:, at:at + wide * CHUNK].rearrange("p (t c) -> p t c", t=wide),
                                   banks[:, bank:bank + wide, :], ACT.Exp, scale=SCALE).then_inc(c.exp_done, 1)

                act.wait_ge(consts, 9)
                act.activation(table_pad[:, :], ones[:, :], ACT.Exp)
                with act.Fori(0, HEADS) as h:
                    for e in range(HE):
                        exps(h, e)
                for e in range(LEAD):
                    exps(HEADS, e)

            attend(first)
            act.wait_ge(flag_ready, 1)
            ok = act.value_load(flag[0:1, 0:1], min_val=0, max_val=P)
            with act.If(ok < P):
                attend(second)
                act.wait_ge(second.exp_done, EXP_0 + HEADS * HE + LEAD)
                act.sem_inc(pass2_end, 1)
                act.wait_ge(pass2_end, 3)

            with act.Fori(0, NT // 4) as g:
                for b in range(2):
                    act.wait_ge(c_turned, g + 2)
                    act.activation(ctxT[:, b, :], banks[:, b, :], ACT.Copy).then_inc(cT_ready, 1)

        @block.vector
        def _(dve):
            links = [0]

            def link(ins):
                links[0] += 1
                ins.then_inc(ln_chain, 1)
                dve.wait_ge(ln_chain, links[0])

            def make_scale(i):
                g, r, s, inv = (fscale[:, i, j:j + 1] for j in range(4))
                link(dve.tensor_scalar(g, amax_all[:, i:i + 1], 1e-12, None, ALU.max))
                link(dve.reciprocal(r, g))
                link(dve.tensor_scalar(s, r, FP8_MAX, FP8_MAX, ALU.mult, ALU.min))
                link(dve.reciprocal(inv, s))

            def quantise(dst, src, s, step):
                y, c, r = (t[:, :] for t in qt)
                step(dve.tensor_scalar(y, src, s, None, ALU.mult))
                step(dve.tensor_scalar(c.bitcast(I32), y.bitcast(I32), EXPONENT_BITS, None, ALU.bitwise_and))
                step(dve.tensor_scalar(c, c, FP8_MIN_NORMAL, ROUND_TO_3_BITS, ALU.max, ALU.mult))
                step(dve.tensor_tensor(r, y, c, ALU.add))
                step(dve.tensor_tensor(y, r, c, ALU.subtract))
                return dve.tensor_scalar(dst, y, FP8_MAX, -FP8_MAX, ALU.min, ALU.max)

            LN_LINKS = 8

            done = [0]

            def ln_step(g, ins):
                done[0] += 1
                ins.then_inc(ln_chain, 1)
                dve.wait_ge(ln_chain, g * LN_LINKS + done[0])

            def row_stats(g):
                done[0] = 0
                for i in range(8):
                    last = dve.bn_stats(stats[:, i, :], x_all[:, bass.ds(g * 8 + i, 1), :].rearrange("p o d -> p (o d)"))
                ln_step(g, last)

            def normalise_rows(g):
                def step(ins):
                    ln_step(g, ins)

                even, odd = stats[:, :, 0:3], stats[:, :, 3:6]
                dve.tensor_tensor(ln[:, 1, :], even[:, :, 1], odd[:, :, 1], ALU.add)
                dve.tensor_tensor(ln[:, 2, :], even[:, :, 1], odd[:, :, 1], ALU.subtract)
                step(dve.tensor_tensor(ln[:, 3, :], even[:, :, 2], odd[:, :, 2], ALU.add))
                dve.tensor_scalar(ln[:, 5, :], ln[:, 1, :], 0.5, None, ALU.mult)
                dve.tensor_tensor(ln[:, 4, :], ln[:, 2, :], ln[:, 2, :], ALU.mult)
                step(dve.tensor_scalar(ln[:, 3, :], ln[:, 3, :], 1.0 / D, EPS, ALU.mult, ALU.add))
                dve.scalar_tensor_tensor(out=ln[:, 0, :], in0=ln[:, 4, :], scalar=0.25, in1=ln[:, 3, :],
                                         op0=ALU.mult, op1=ALU.add).then_inc(var_ready, 1)
                dve.wait_ge(root_ready, g + 1)
                step(dve.reciprocal(ln[:, 2, :], ln[:, 1, :]))
                step(dve.tensor_tensor(ln[:, 3, :], ln[:, 2, :], ln[:, 2, :], ALU.mult))
                step(dve.tensor_tensor(ln[:, 3, :], ln[:, 3, :], ln[:, 0, :], ALU.mult))
                step(dve.tensor_scalar(ln[:, 3, :], ln[:, 3, :], -0.5, 1.5, ALU.mult, ALU.add))
                step(dve.tensor_tensor(ln[:, 4, :], ln[:, 2, :], ln[:, 3, :], ALU.mult))
                for i in range(8):
                    tile = bass.ds(g * 8 + i, 1)
                    last = dve.tensor_scalar(xn_all[:, tile, :], x_all[:, tile, :], ln[:, 5, i:i + 1],
                                             ln[:, 4, i:i + 1], ALU.subtract, ALU.mult)
                    if i == CT - 1 and isinstance(g, int) and g == 0:
                        last.then_inc(xn_first, 1)
                last.then_inc(xn_ready, 1)
                assert done[0] == LN_LINKS

            def remainders(n, par, half, outputs=(0, 1)):
                for o in outputs:
                    bank, buf = term(o, par)
                    dve.wait_ge(lo_done, n * 2 + (LO_0 - 2 + o + 1))
                    dve.wait_ge(hi_done, n * 2 + (o + 1))
                    dve.scalar_tensor_tensor(out=rest[o][:, :], in0=banks[:, bank, :],
                                             scalar=qk_bias[:, o, half:half + 1], in1=buf[:, 0, :],
                                             op0=ALU.add, op1=ALU.subtract).then_inc(rest_done, 1)

            def values(n):
                for b in range(2):
                    dve.wait_ge(v_mm, n * 2 + (b + 1))
                    dve.tensor_tensor(v_all[:, bass.ds(n * CT + 2 * b, 2), :],
                                      banks[:, 6 + b, :].rearrange("p (t d) -> p t d", t=2), bv_sb[:, :, :],
                                      ALU.add).then_inc(v_done, 1)

            dve.wait_ge(x_in[0], 16 * 4)
            row_stats(0)
            normalise_rows(0)
            dve.wait_ge(x_in[1], 16 * 3)
            with dve.Fori(0, NCH // 2 - 1) as cc:
                row_stats(cc + 1)
                normalise_rows(cc + 1)
                remainders(cc * 2, 0, 0)
                values(cc * 2)
                remainders(cc * 2 + 1, 1, 0)
                values(cc * 2 + 1)
            for par in range(2):
                remainders(NCH - 2 + par, par, 0)
                values(NCH - 2 + par)
            links[0] = LN_LINKS * 4
            wf_flat = w_sb["f"][:, :, :].rearrange("p k n -> p (k n)")

            def largest_of_x(g):
                link(dve.tensor_reduce(amax[:, 0, g:g + 1], xn_all[:, g * 8:(g + 1) * 8, :], AX.XY, ALU.max,
                                       apply_absolute_value=True))

            def largest():
                dve.wait_ge(w_in["f"], 16)
                dve.tensor_reduce(amax[:, 0, 7:8], amax[:, 0, 0:4], AX.X, ALU.max)
                dve.tensor_reduce(amax[:, 1, 7:8], wf_flat, AX.X, ALU.max, apply_absolute_value=True
                                  ).then_inc(amax_ready, 1)
            def quantise_weight():
                dve.wait_ge(lo_done, LO_0 + 4 * NCH)
                quantise(w8T[:, :, :].rearrange("p k n -> p (k n)"), wf_flat, fscale[:, 1, 2:3], link
                         ).then_inc(xq_used, 1)
                dve.wait_ge(xq_used, 1)

            QUANT_STEPS = 6
            qn = [0]

            def attend(c):
                MAX_LINKS = 4 + c.full * UT
                SUM_LINKS = 2 if c.full else 3
                HEAD_LINKS = 2 * (MAX_LINKS + SUM_LINKS)

                def chain(ins, count):
                    ins.then_inc(c.chain, 1)
                    dve.wait_ge(c.chain, count)

                def maxima(job0, link0):
                    if c.full:
                        with dve.Fori(0, UT) as i:
                            for kb in range(S // CHUNK):
                                dve.wait_ge(c.misc_full, i * (S // CHUNK) + (job0 + kb + 1))
                                dve.tensor_reduce(mpart[:, kb:kb + 1], misc, AX.X, ALU.max).then_inc(c.misc_free, 1)
                            dve.wait_ge(c.misc_free, i * (S // CHUNK) + (job0 + S // CHUNK))
                            chain(dve.tensor_reduce(mcol[:, bass.ds(i, 1)], mpart[:, :], AX.X, ALU.max),
                                  i + (link0 + 1))
                        link0 = link0 + UT
                    else:
                        for j in range(c.max_jobs):
                            some_maxima(j, job0)
                        dve.wait_ge(c.misc_free, job0 + c.max_jobs)
                    minus_maxima(job0 + c.max_jobs, link0)

                def some_maxima(j, job0):
                    dve.wait_ge(c.misc_full, job0 + (j + 1))
                    dve.tensor_reduce(mcol[:, JT * j:JT * (j + 1)], misc.rearrange("p (t k) -> p t k", t=JT),
                                      AX.X, ALU.max).then_inc(c.misc_free, 1)

                def minus_maxima(job, link0):
                    negate(link0)
                    to_rows(job)

                def negate(link0):
                    above = 0.0 if c.full else HEADROOM / SCALE
                    chain(dve.tensor_scalar(neg_full[:, :], mcol[:, :], -1.0, -above, ALU.mult, ALU.add), link0 + 1)
                    chain(dve.tensor_copy(neg[:, 0, :], neg_full[:, :]), link0 + 2)
                    chain(dve.tensor_tensor(neg_rest[:, :], neg_full[:, :], neg[:, 0, :], ALU.subtract), link0 + 3)
                    chain(dve.tensor_copy(neg[:, 1, :], neg_rest[:, :]), link0 + 4)
                    dve.tensor_tensor(neg[:, 2, :], neg_rest[:, :], neg[:, 1, :], ALU.subtract).then_inc(c.neg_ready, 1)

                def to_rows(job):
                    dve.wait_ge(c.misc_full, job + 1)
                    dve.tensor_copy(neg_row[:, :], misc.bitcast(BF16)[0:PARTS * UT, 0:P]
                                    ).then_inc(c.row_ready, 1)
                    dve.wait_ge(c.row_ready, neg_count[0])
                    dve.sem_inc(c.misc_free, 1)

                neg_count = [1]

                def take_sums(h, u, link0):
                    dve.wait_ge(c.pv_done, h * STEPS + (PV_0 + (u + 1) * KT))
                    dve.transpose(o_sb[:, :], acc).then_inc(c.acc_free, 1)
                    dve.wait_ge(c.acc_free, h * 2 + (u + 1 + ACC_0))
                    if not c.full:
                        chain(dve.scalar_tensor_tensor(out=o_junk[:, :], in0=o_sb[:, :], scalar=OVERFLOW_MARGIN,
                                                       in1=zeros[:, :].to_broadcast([P, CHUNK]), op0=ALU.mult,
                                                       op1=ALU.mult, accum_out=o_inf[:, bass.ds(h * 2 + u, 1)]),
                              link0 + 1)

                def normalise(h, u, link0):
                    sums = o_sb[:, :].rearrange("p (t v) -> p t v", v=VCOLS)
                    chain(dve.reciprocal(rden[:, :], sums[:, :, DH]), link0 + 1)
                    dst = ctx_all.rearrange("p (c u i) d -> p c u i d", u=UNITS, i=CT)
                    for cc in range(NCH // 2):
                        tiles = slice(cc * CT, (cc + 1) * CT)
                        last = dve.tensor_tensor(dst[:, cc, u, :, bass.ds(h * DH, DH)], sums[:, tiles, 0:DH],
                                                 rden[:, tiles].unsqueeze(2).to_broadcast([P, CT, DH]), ALU.mult)
                    last.then_inc(c.chain, 1)

                if not c.full:
                    for n in range(NCH):
                        if n == TURN_FIRST:
                            dve.wait_ge(c.misc_free, c.max_jobs)
                            negate(0)
                        remainders(NCH + n, n % 2, 1, (0,))
                        if n == TURN_FIRST:
                            to_rows(c.max_jobs)
                        remainders(NCH + n, n % 2, 1, (1,))
                        if n in FIRST_MAX:
                            some_maxima(FIRST_MAX[n], 0)
                        if n < 4:
                            largest_of_x(n)
                    largest()
                    dve.wait_ge(amax_shared, 1)
                    make_scale(0)
                    make_scale(1)
                    link(dve.tensor_tensor(out_scale[:, :], fscale[:, 0, 3:4], fscale[:, 1, 3:4], ALU.mult))
                    quantise_weight()
                else:
                    maxima(0, 0)
                JOB0 = c.max_jobs + 1
                with dve.Fori(0, HEADS) as h:
                    job = h * c.head_jobs + JOB0
                    lk = h * HEAD_LINKS + MAX_LINKS
                    neg_count[0] = h * 2 + 2
                    maxima(job, lk)
                    take_sums(h, 0, lk + MAX_LINKS)
                    normalise(h, 0, lk + (MAX_LINKS + SUM_LINKS - 2))
                    if not c.full:
                        dve.wait_ge(xq_in, h * 16 + 16)
                        qn[0] = 0

                        def qstep(ins):
                            qn[0] += 1
                            ins.then_inc(quant_chain, 1)
                            dve.wait_ge(quant_chain, h * QUANT_STEPS + qn[0])

                        quantise(x8T[:, :, :].rearrange("p k s -> p (k s)")[:, bass.ds(h * CHUNK, CHUNK)], xq,
                                 fscale[:, 0, 2:3], qstep).then_inc(xq_used, 1)
                        two = x_all[:, bass.ds(h * 2, 2), :]
                        qstep(dve.tensor_tensor(two, two, bo_sb[:, :, :], ALU.add))
                    neg_count[0] = h * 2 + 3
                    lk = lk + (MAX_LINKS + SUM_LINKS)
                    maxima(job + (c.max_jobs + 1), lk)
                    take_sums(h, 1, lk + MAX_LINKS)
                    normalise(h, 1, lk + (MAX_LINKS + SUM_LINKS - 2))

                dve.wait_ge(c.chain, HEADS * HEAD_LINKS + MAX_LINKS)

            attend(first)
            link(dve.tensor_reduce(all_ok[:, 0:1], o_inf[:, :], AX.X, ALU.add))
            dve.tensor_scalar(all_ok[:, 1:2], all_ok[:, 0:1], 0.0, None, ALU.is_equal).then_inc(flag_ok, 1)
            dve.wait_ge(flag_sum, 1)
            dve.tensor_copy(flag[0:1, 0:1], misc[0:1, 0:1]).then_inc(flag_ready, 1)
            dve.wait_ge(flag_ready, 1)
            ok = dve.value_load(flag[0:1, 0:1], min_val=0, max_val=P)
            with dve.If(ok < P):
                attend(second)
                dve.wait_ge(second.misc_free, HEADS * second.head_jobs + second.max_jobs + 1)
                dve.sem_inc(pass2_end, 1)
                dve.wait_ge(pass2_end, 3)

            with dve.Fori(0, NT // 4) as g:
                for b in range(2):
                    dve.wait_ge(out_ready, g * 2 + (b + 1))
                    dve.wait_ge(ffn_done, g * 2 + (b + 1))
                    dve.scalar_tensor_tensor(out=y_sb[b], in0=banks[:, 4 + b, :], scalar=out_scale[:, 0:1],
                                             in1=bf_sb[:, :, :].rearrange("p t d -> p (t d)"), op0=ALU.mult,
                                             op1=ALU.add).then_inc(y_done, 1)
                for b in range(2):
                    dve.wait_ge(proj_done, g * 2 + (b + 1))
                    dve.tensor_tensor(res[b][:, :].rearrange("p (t d) -> p t d", t=2),
                                      banks[:, 2 + b, :].rearrange("p (t d) -> p t d", t=2),
                                      x_all[:, bass.ds(g * 4 + 2 * b, 2), :], ALU.add).then_inc(res_done, 1)
                    dve.wait_ge(res_done, g * 2 + (b + 1 + 2))
                    dve.wait_ge(y_done, g * 2 + (2 + 2))
                    dve.wait_ge(out_saved[b], g * 16 + OUT_0)
                    dve.tensor_tensor(o_out[b][:, :], res[b][:, :], y_sb[b], ALU.add).then_inc(out_ready, 1)

        @block.tensor
        def _(pe):
            pe.wait_ge(consts, 9)
            for n in "qkv":
                pe.wait_ge(w_in[n], 16)

            def turn(n, par):
                pe.wait_ge(xnc_ready, n)
                turn_tiles(xnc[par])

            def turn_tiles(src):
                for k in range(KD):
                    for j in range(CT):
                        last = pe.transpose(banks[:, k, j * P:(j + 1) * P], src[:, j, k * P:(k + 1) * P],
                                            ident[:, :])
                    last.then_inc(turned, 1)

            def chunk_columns(xT, o):
                return xT.rearrange("f (i j p) -> f j i p", i=CT, j=QB) if o == 0 else xT

            def project(n, par, half, xT, outputs=(0, 1)):
                for o in outputs:
                    pe.wait_ge(rest_done, n * 2 + (REST_0 - 4 + o + 1))
                    for k in range(KD):
                        last = pe.matmul(banks[:, term(o, par)[0], :],
                                         w_sb["qk"[o]][:, k, half * P:(half + 1) * P],
                                         chunk_columns(xT[:, k, :], o), start=(k == 0), stop=(k == KD - 1))
                    last.then_inc(qk_done, 1)

            def project_v(n, par):
                for b in range(2):
                    pe.wait_ge(v_done, n * 2 + (V_0 - 2 + b + 1))
                    for j in range(2):
                        for k in range(KD):
                            t = 2 * b + j
                            last = pe.matmul(banks[:, 6 + b, j * D:(j + 1) * D],
                                             xnTc[par][:, k, t * P:(t + 1) * P], w_sb["v"][:, k, :],
                                             start=(k == 0), stop=(k == KD - 1))
                    last.then_inc(v_mm, 1)

            def group(cc, last):
                for par in range(2):
                    n = cc * 2 + par
                    pe.wait_ge(xT_ready, n * 2 + 2)
                    project(n, par, 0, xnTc[par])
                    if not (last and par):
                        turn(n + 1, 1 - par)
                    project_v(n, par)

            pe.wait_ge(xn_first, 1)
            turn_tiles(xn_all)
            with pe.Fori(0, NCH // 2 - 1) as cc:
                group(cc, False)
            group(NCH // 2 - 1, True)
            def attend(c):
                def misc_job(job, ready):
                    if ready:
                        pe.wait_ge(c.misc_free, job)

                def max_job(u, j, job, ready=True):
                    misc_job(job, ready)
                    for i in range(JT):
                        at = u * UQ + (JT * j + i) * P
                        last = pe.matmul(misc[:, i * AK:(i + 1) * AK], q_st[0:KROWS, at:at + P], k_st[0:KROWS, 0:AK],
                                         start=True, stop=True)
                    last.then_inc(c.misc_full, 1)

                def all_max_jobs(u, job0, loads):
                    with pe.Fori(0, UT) as i:
                        for s in (c.q_in[u], *c.k_in):
                            pe.wait_ge(s, loads)
                        for kb in range(S // CHUNK):
                            pe.wait_ge(c.misc_free, i * (S // CHUNK) + (job0 + kb))
                            pe.matmul(misc, q_st[0:KROWS, bass.ds(i * P + u * UQ, P)],
                                      k_st[0:KROWS, kb * CHUNK:(kb + 1) * CHUNK], start=True, stop=True
                                      ).then_inc(c.misc_full, 1)

                def turn_maxima(job, count):
                    misc_job(job, True)
                    pe.wait_ge(c.neg_ready, count)
                    pe.transpose(misc.bitcast(BF16)[:, 0:P], neg[:, :, :].rearrange("p a t -> p (a t)"),
                                 ident_bf[:, :]).then_inc(c.misc_full, 1)

                def scores(h, e, before_unit=None):
                    nxt, e = divmod(e, HE)
                    u, r0 = e // UE, e % UE * WIDE
                    blocks = q_st[:, u * UQ:(u + 1) * UQ].rearrange("k (c j x) -> k j c x", j=QB, x=P)
                    if r0 == 0:
                        if before_unit:
                            before_unit(u, nxt)
                        pe.wait_ge(c.row_in[u], h * 48 + 48 * (1 + nxt))
                        pe.wait_ge(c.q_in[u], h * (16 * TERMS) + 16 * TERMS * (1 + nxt))
                    pe.wait_ge(c.exp_done, h * HE + (EXP_0 + nxt * HE + e - banks_user(e) + 1))
                    for r in range(r0, min(r0 + WIDE, UT4)):
                        kt, qb = divmod(r, QB)
                        if u == 0 and r % (UT4 // 2) == 0:
                            pe.wait_ge(c.k_in[r // (UT4 // 2)], h * (16 * TERMS) + 16 * TERMS * (1 + nxt))
                        last = pe.matmul(banks[:, WIDE * (e % BUFS) + r - r0, :], k_st[:, kt * P:(kt + 1) * P],
                                         blocks[:, qb],
                                         start=True, stop=True)
                    last.then_inc(c.st_done, 1)

                def weighted_sum(h, t):
                    u, kt = divmod(t, KT)
                    if kt == 0:
                        pe.wait_ge(c.acc_free, h * 2 + (u + ACC_0))
                    if u == 0 and kt % (KT // 2) == 0:
                        pe.wait_ge(c.v_in[kt // (KT // 2)], h + 1)
                    pe.wait_ge(c.exp_done, h * HE + (EXP_0 + exp_of(QB * t + QB - 1)[0] + 1))
                    for qb in range(QB):
                        at = (QB * kt + qb) % RING * CHUNK
                        last = pe.matmul(banks[VCOLS * qb:VCOLS * (qb + 1), 6, :], v_st[:, kt, :],
                                         probs[:, at:at + CHUNK],
                                         start=(kt == 0), stop=(kt == KT - 1), tile_position=(0, VCOLS * qb))
                    last.then_inc(c.pv_done, 1)

                if c.full:
                    with pe.Fori(0, UT) as i:
                        for s in (c.q_in[0], *c.k_in):
                            pe.wait_ge(s, 16 * TERMS)
                        for kb in range(S // CHUNK):
                            if kb:
                                pe.wait_ge(c.misc_free, i * (S // CHUNK) + kb)
                            pe.matmul(misc, q_st[0:KROWS, bass.ds(i * P, P)],
                                      k_st[0:KROWS, kb * CHUNK:(kb + 1) * CHUNK], start=True, stop=True
                                      ).then_inc(c.misc_full, 1)
                        pe.wait_ge(c.misc_free, i * (S // CHUNK) + S // CHUNK)
                    turn_maxima(c.max_jobs, 1)
                else:
                    for n in range(NCH):
                        pe.wait_ge(xT_back[n % 4], 16 * (n // 4 + 1))
                        project(NCH + n, n % 2, 1, xnT_again[n % 4], (0,))
                        if n == TURN_FIRST:
                            turn_maxima(c.max_jobs, 1)
                        project(NCH + n, n % 2, 1, xnT_again[n % 4], (1,))
                        if n in FIRST_MAX:
                            j = FIRST_MAX[n]
                            if j == 0:
                                pe.wait_ge(c.q_in[0], 16 * TERMS)
                                pe.wait_ge(c.k_in[0], 16 * TERMS)
                                pe.wait_ge(v_done, V_0 + 2 * NCH)
                            max_job(0, j, j, ready=j > 0)
                JOB0 = c.max_jobs + 1
                for e in range(LEAD):
                    if e in (1, 2) and not c.full:
                        pe.wait_ge(rest_done, REST_0 + 4 * NCH - 2 * (2 - e))
                    scores(0, e)

                with pe.Fori(0, HEADS) as h:
                    job = h * c.head_jobs + JOB0
                    def at(t):
                        return exp_of(QB * t)[0]

                    jobs = {}
                    if not c.full:
                        for j in range(c.max_jobs):
                            jobs[at(14 + 4 * j)] = lambda j=j: max_job(1, j, job + j)
                            jobs[at(51 + 2 * j)] = lambda j=j: max_job(0, j, job + (c.max_jobs + 1 + j))
                        jobs[at(22)] = lambda: turn_maxima(job + c.max_jobs, h * 2 + 2)
                        jobs[at(57)] = lambda: turn_maxima(job + (2 * c.max_jobs + 1), h * 2 + 3)

                    def maximum_first(u, nxt):
                        j0 = job if u else job + (c.max_jobs + 1)
                        all_max_jobs(u, j0, h * (16 * TERMS) + 16 * TERMS * (1 + nxt))
                        turn_maxima(j0 + c.max_jobs, h * 2 + (2 if u else 3))

                    for e in range(HE):
                        scores(h, e + LEAD, maximum_first if c.full else None)
                        if not c.full and e in (at(14), at(51)):
                            pe.wait_ge(c.q_in[e < UE], h * (16 * TERMS) + 16 * TERMS * (1 + (e >= UE)))
                            pe.wait_ge(c.k_in[0], h * (16 * TERMS) + 16 * TERMS * (1 + (e >= UE)))
                        if e in jobs:
                            jobs[e]()
                        for t in range(STEPS):
                            if exp_of(QB * t + QB - 1)[0] == e:
                                weighted_sum(h, t)
                pe.wait_ge(c.exp_done, EXP_0 + HEADS * HE + LEAD)

            attend(first)
            pe.wait_ge(first.misc_free, HEADS * first.head_jobs + first.max_jobs + 1)
            pe.wait_ge(flag_ok, 1)
            pe.matmul(misc[0:1, 0:1], all_ok[:, 1:2], ones[:, :], start=True, stop=True).then_inc(flag_sum, 1)
            pe.wait_ge(flag_ready, 1)
            ok = pe.value_load(flag[0:1, 0:1], min_val=0, max_val=P)
            with pe.If(ok < P):
                attend(second)
                pe.wait_ge(second.misc_free, HEADS * second.head_jobs + second.max_jobs + 1)
                pe.sem_inc(pass2_end, 1)
                pe.wait_ge(pass2_end, 3)

            pe.wait_ge(w_in["o"], 16)
            with pe.Fori(0, NT // 4) as g:
                pe.wait_ge(cx_ready, g + 1)
                for b in range(2):
                    for j in range(2):
                        for k in range(KD):
                            last = pe.transpose(banks[:, b, (2 * k + j) * P:(2 * k + j + 1) * P],
                                                cx[:, 2 * b + j, k * P:(k + 1) * P], ident[:, :])
                last.then_inc(c_turned, 1)
                for b in range(2):
                    pe.wait_ge(y_done, g * 2 + (b + 1))
                    for j in range(2):
                        for k in range(KD):
                            last = pe.matmul(banks[:, 4 + b, j * D:(j + 1) * D],
                                             x8T[:, k, bass.ds(g * (4 * P) + (2 * b + j) * P, P)], w8T[:, k, :],
                                             start=(k == 0), stop=(k == KD - 1))
                    last.then_inc(ffn_done, 1)
                for b in range(2):
                    pe.wait_ge(cT_ready, g * 2 + (b + 1))
                    pe.wait_ge(res_done, g * 2 + (b + 1))
                    for j in range(2):
                        for k in range(KD):
                            last = pe.matmul(banks[:, 2 + b, j * D:(j + 1) * D],
                                             ctxT[:, b, (2 * k + j) * P:(2 * k + j + 1) * P], w_sb["o"][:, k, :],
                                             start=(k == 0), stop=(k == KD - 1))
                    last.then_inc(proj_done, 1)


_INS = ["L0_attn_query", "L0_attn_q_w", "L0_attn_q_b", "L0_attn_k_w", "L0_attn_k_b", "L0_attn_v_w", "L0_attn_v_b",
        "L0_attn_out_w", "L0_attn_out_b", "L0_ffn_weight", "L0_ffn_bias"]


def kernel(**inputs):
    import numpy as _np
    import concourse.bacc as _bacc
    from concourse import mybir as _mybir
    from concourse.bass_utils import run_bass_kernel_spmd as _run

    nc = _bacc.Bacc("TRN2", target_bir_lowering=False, num_devices=1)
    arrays, args = {}, []
    for name in _INS:
        a = _np.asarray(inputs[name])
        if name.endswith("_w") or name.endswith("weight"):
            a = a.T
        a = _np.ascontiguousarray(a)
        arrays[f"in_{name}_dram"] = a
        args.append(nc.dram_tensor(f"in_{name}_dram", a.shape, _mybir.dt.from_np(a.dtype), kind="ExternalInput").ap())
    shape = inputs["L0_attn_query"].shape
    args.append(nc.dram_tensor("out_0_dram", shape, _mybir.dt.float32, kind="ExternalOutput").ap())
    program(nc, *args)
    r = _run(nc, [arrays], core_ids=[0])
    return r.results[0]["out_0_dram"]
```
